# Optimizing a Trainium2 kernel written in Bass

```python
import numpy as np
import jax
import jax.numpy as jnp

def _softmax(x, axis=-1):
    return jax.nn.softmax(x, axis=axis)

def _gelu(x):
    return jax.nn.gelu(x, approximate=True)

def _silu(x):
    return jax.nn.silu(x)

def _sigmoid(x):
    return jax.nn.sigmoid(x)

def _layernorm(x, axis=-1, eps=1e-05):
    m = jnp.mean(x, axis=axis, keepdims=True)
    v = jnp.var(x, axis=axis, keepdims=True)
    return (x - m) / jnp.sqrt(v + eps)

def _scatter_add(tgt, idx, src, axis=0):
    return tgt.at[idx].add(src)

def _segment_sum(src, seg, n):
    return jax.ops.segment_sum(src, seg, n)
kernel_name = 'mk_vit_tower_d1_tok_img1024_r4_cfa266'

def setup_inputs(seed: int=0):
    np.random.seed(seed)
    _w = jnp.asarray

    def _rec_inputs():
        import jax
        import jax.numpy as jnp
        _rk = jax.random.key(seed)
        x = -0.00016672 + 0.999947 * jax.random.normal(jax.random.fold_in(_rk, 1), (64, 3, 96, 96), jnp.float32)
        return x
    x = _rec_inputs()

    def _L0_tok_setup():
        import jax, jax.numpy as jnp
        import numpy as np
        EPS = 1e-05

        def _layernorm(x, w, b):
            mu = jnp.mean(x, axis=-1, keepdims=True)
            var = jnp.mean(jnp.square(x - mu), axis=-1, keepdims=True)
            return (x - mu) * jax.lax.rsqrt(var + EPS) * w + b
        key = jax.random.key(seed)
        ks = jax.random.split(key, 8)
        B, C, H, W = (64, 3, 96, 96)
        P, D = (16, 256)
        patch_dim = C * P * P
        num_patches = H // P * (W // P)
        x = jax.random.normal(ks[0], (B, C, H, W), dtype=jnp.float32)
        ln1_w = jnp.ones((patch_dim,), jnp.float32)
        ln1_b = jnp.zeros((patch_dim,), jnp.float32)
        lin_w = jax.random.normal(ks[1], (patch_dim, D), jnp.float32) / np.sqrt(patch_dim)
        lin_b = jnp.zeros((D,), jnp.float32)
        ln2_w = jnp.ones((D,), jnp.float32)
        ln2_b = jnp.zeros((D,), jnp.float32)
        pos_embedding = jax.random.normal(ks[2], (1, num_patches + 1, D), jnp.float32)
        cls_token = jax.random.normal(ks[3], (1, 1, D), jnp.float32)
        return dict(x=x, ln1_w=ln1_w, ln1_b=ln1_b, lin_w=lin_w, lin_b=lin_b, ln2_w=ln2_w, ln2_b=ln2_b, pos_embedding=pos_embedding, cls_token=cls_token)
    _L0_tok_all = _L0_tok_setup()
    _L0_tok_in = {k: v for k, v in _L0_tok_all.items() if k in ('ln1_w', 'ln1_b', 'lin_w', 'lin_b', 'ln2_w', 'ln2_b', 'pos_embedding', 'cls_token')}
    del _L0_tok_all

    def _L0_attn_setup():
        import jax, jax.numpy as jnp
        import numpy as np
        DIM = 256
        HEADS = 16
        HEAD_DIM = DIM // HEADS
        SCALE = float(HEAD_DIM ** (-0.25))
        ROPE_BASE = 10000.0

        def apply_rope(x):
            B, N, H, D = x.shape
            half = D // 2
            inv_freq = 1.0 / ROPE_BASE ** (jnp.arange(half, dtype=jnp.float32) / half)
            freqs = jnp.arange(N, dtype=jnp.float32)[:, None] * inv_freq[None, :]
            cos = jnp.cos(freqs)[None, :, None, :].astype(x.dtype)
            sin = jnp.sin(freqs)[None, :, None, :].astype(x.dtype)
            x1, x2 = (x[..., :half], x[..., half:])
            return jnp.concatenate([x1 * cos - x2 * sin, x1 * sin + x2 * cos], axis=-1)
        key = jax.random.key(seed)
        k1, k2, k3 = jax.random.split(key, 3)
        x = jax.random.normal(k1, (4, 1024, DIM), dtype=jnp.float32)
        w_qkv = jax.random.normal(k2, (DIM, 3 * DIM), dtype=jnp.float32) * 0.02
        w_out = jax.random.normal(k3, (DIM, DIM), dtype=jnp.float32) * 0.02
        return {'x': x, 'w_qkv': w_qkv, 'w_out': w_out}
    _L0_attn_all = _L0_attn_setup()
    _L0_attn_in = {k: v for k, v in _L0_attn_all.items() if k in ('w_qkv', 'w_out')}
    del _L0_attn_all

    def _L0_ffn_setup():
        import jax, jax.numpy as jnp
        import numpy as np
        B, T, C, H, E = (4, 512, 256, 512, 8)
        CAPACITY_FACTOR = 1.0
        key = jax.random.key(seed)
        ks = jax.random.split(key, 5)
        scale = 0.02
        return {'x': jax.random.normal(ks[0], (B, T, C), dtype=jnp.float32), 'Wg': jax.random.normal(ks[1], (E, C), dtype=jnp.float32) * scale, 'W1': jax.random.normal(ks[2], (E, H, C), dtype=jnp.float32) * scale, 'W2': jax.random.normal(ks[3], (E, C, H), dtype=jnp.float32) * scale, 'W3': jax.random.normal(ks[4], (E, H, C), dtype=jnp.float32) * scale}
    _L0_ffn_all = _L0_ffn_setup()
    _L0_ffn_in = {k: v for k, v in _L0_ffn_all.items() if k in ('Wg', 'W1', 'W2', 'W3')}
    del _L0_ffn_all
    return {'x': x, 'L0_tok_ln1_w': _L0_tok_in['ln1_w'], 'L0_tok_ln1_b': _L0_tok_in['ln1_b'], 'L0_tok_lin_w': _L0_tok_in['lin_w'], 'L0_tok_lin_b': _L0_tok_in['lin_b'], 'L0_tok_ln2_w': _L0_tok_in['ln2_w'], 'L0_tok_ln2_b': _L0_tok_in['ln2_b'], 'L0_tok_pos_embedding': _L0_tok_in['pos_embedding'], 'L0_tok_cls_token': _L0_tok_in['cls_token'], 'L0_attn_w_qkv': _L0_attn_in['w_qkv'], 'L0_attn_w_out': _L0_attn_in['w_out'], 'L0_ffn_Wg': _L0_ffn_in['Wg'], 'L0_ffn_W1': _L0_ffn_in['W1'], 'L0_ffn_W2': _L0_ffn_in['W2'], 'L0_ffn_W3': _L0_ffn_in['W3']}

def reference(x, L0_tok_ln1_w, L0_tok_ln1_b, L0_tok_lin_w, L0_tok_lin_b, L0_tok_ln2_w, L0_tok_ln2_b, L0_tok_pos_embedding, L0_tok_cls_token, L0_attn_w_qkv, L0_attn_w_out, L0_ffn_Wg, L0_ffn_W1, L0_ffn_W2, L0_ffn_W3):
    import jax
    import jax.numpy as jnp

    def _L0_tok_ref(x, ln1_w, ln1_b, lin_w, lin_b, ln2_w, ln2_b, pos_embedding, cls_token):
        import jax, jax.numpy as jnp
        import numpy as np
        EPS = 1e-05

        def _layernorm(x, w, b):
            mu = jnp.mean(x, axis=-1, keepdims=True)
            var = jnp.mean(jnp.square(x - mu), axis=-1, keepdims=True)
            return (x - mu) * jax.lax.rsqrt(var + EPS) * w + b
        B, C, H, W = x.shape
        P = 16
        h, w = (H // P, W // P)
        patches = x.reshape(B, C, h, P, w, P)
        patches = patches.transpose(0, 2, 4, 3, 5, 1)
        patches = patches.reshape(B, h * w, P * P * C)
        y = _layernorm(patches, ln1_w, ln1_b)
        y = jnp.einsum('bnp,pd->bnd', y, lin_w) + lin_b
        y = _layernorm(y, ln2_w, ln2_b)
        cls = jnp.broadcast_to(cls_token, (B, 1, y.shape[-1]))
        y = jnp.concatenate([cls, y], axis=1)
        n = h * w
        y = y + pos_embedding[:, :n + 1]
        return y

    def _L0_attn_ref(x, w_qkv, w_out):
        import jax, jax.numpy as jnp
        import numpy as np
        DIM = 256
        HEADS = 16
        HEAD_DIM = DIM // HEADS
        SCALE = float(HEAD_DIM ** (-0.25))
        ROPE_BASE = 10000.0

        def apply_rope(x):
            B, N, H, D = x.shape
            half = D // 2
            inv_freq = 1.0 / ROPE_BASE ** (jnp.arange(half, dtype=jnp.float32) / half)
            freqs = jnp.arange(N, dtype=jnp.float32)[:, None] * inv_freq[None, :]
            cos = jnp.cos(freqs)[None, :, None, :].astype(x.dtype)
            sin = jnp.sin(freqs)[None, :, None, :].astype(x.dtype)
            x1, x2 = (x[..., :half], x[..., half:])
            return jnp.concatenate([x1 * cos - x2 * sin, x1 * sin + x2 * cos], axis=-1)
        B, N, D = x.shape
        qkv = x @ w_qkv
        q, k, v = jnp.split(qkv, 3, axis=-1)
        q = q.reshape(B, N, HEADS, HEAD_DIM)
        k = k.reshape(B, N, HEADS, HEAD_DIM)
        v = v.reshape(B, N, HEADS, HEAD_DIM)
        q = apply_rope(q)
        k = apply_rope(k)
        q = jax.nn.elu(q * SCALE) + 1.0
        k = jax.nn.elu(k * SCALE) + 1.0
        qT = jnp.moveaxis(q, 1, 0)
        kT = jnp.moveaxis(k, 1, 0)
        vT = jnp.moveaxis(v, 1, 0)
        kv0 = jnp.zeros((B, HEADS, HEAD_DIM, HEAD_DIM), dtype=q.dtype)
        ks0 = jnp.zeros((B, HEADS, HEAD_DIM), dtype=q.dtype)

        def step(carry, qkv_t):
            kv, ks = carry
            qt, kt, vt = qkv_t
            kv = kv + jnp.einsum('bhd,bhm->bhdm', kt, vt)
            ks = ks + kt
            denom = jnp.maximum(jnp.einsum('bhd,bhd->bh', qt, ks), 1e-06)
            out_t = jnp.einsum('bhd,bhdm->bhm', qt, kv) / denom[..., None]
            return ((kv, ks), out_t)
        _, outT = jax.lax.scan(step, (kv0, ks0), (qT, kT, vT))
        out = jnp.moveaxis(outT, 0, 1).reshape(B, N, D)
        return out @ w_out

    def _L0_ffn_ref(x, Wg, W1, W2, W3):
        import jax, jax.numpy as jnp
        import numpy as np
        B, T, C, H, E = (4, 512, 256, 512, 8)
        CAPACITY_FACTOR = 1.0
        b, t, c = x.shape
        e = Wg.shape[0]
        n = b * t
        capacity = max(1, int(CAPACITY_FACTOR * n / e))
        x_flat = x.reshape(n, c)
        scores = (x_flat @ Wg.T).T
        top_vals, token_idx = jax.lax.top_k(scores, capacity)
        token_w = jax.nn.softmax(top_vals, axis=-1)
        xg = x_flat[token_idx]
        h = jax.nn.silu(jnp.einsum('eic,ehc->eih', xg, W1)) * jnp.einsum('eic,ehc->eih', xg, W3)
        y = jnp.einsum('eih,ech->eic', h, W2) * token_w[..., None]
        out = jnp.zeros_like(x_flat).at[token_idx.reshape(-1)].add(y.reshape(-1, c))
        return out.reshape(b, t, c)
    h = _L0_tok_ref(x, L0_tok_ln1_w, L0_tok_ln1_b, L0_tok_lin_w, L0_tok_lin_b, L0_tok_ln2_w, L0_tok_ln2_b, L0_tok_pos_embedding, L0_tok_cls_token)
    h = h + _L0_attn_ref(_layernorm(h, axis=-1), L0_attn_w_qkv, L0_attn_w_out)
    h = h + _L0_ffn_ref(_layernorm(h, axis=-1), L0_ffn_Wg, L0_ffn_W1, L0_ffn_W2, L0_ffn_W3)
    return h

_drawn_inputs = setup_inputs


def setup_inputs(seed=0):
    import zlib

    import numpy as np

    out = dict(_drawn_inputs(seed))
    spreads = {'L0_tok_ln1_w': (1.0, 0.2),
     'L0_tok_ln1_b': (0.0, 0.1),
     'L0_tok_lin_b': (0.0, 0.1),
     'L0_tok_ln2_w': (1.0, 0.2),
     'L0_tok_ln2_b': (0.0, 0.1)}
    factors = {'L0_ffn_Wg': 8.0, 'L0_ffn_W1': 8.0, 'L0_ffn_W2': 8.0, 'L0_ffn_W3': 8.0}
    for name, (base, spread) in spreads.items():
        noise = np.random.default_rng([zlib.crc32(name.encode()), seed]).standard_normal(out[name].shape)
        drawn = base * np.exp(spread * noise) if base else spread * noise
        out[name] = jnp.asarray(drawn.astype(out[name].dtype))
    for name, factor in factors.items():
        out[name] = (out[name] * factor).astype(out[name].dtype)
    return out
```

```python
from contextlib import ExitStack

import concourse.bass as bass
from concourse import mybir

F32 = mybir.dt.float32
BF16 = mybir.dt.bfloat16
I32 = mybir.dt.int32
U32 = mybir.dt.uint32
ALU = mybir.AluOpType
ACT = mybir.ActivationFunctionType
AX = mybir.AxisListType

P = 128
BATCH = 64
SEQ = 37
IMGS = 3
T = IMGS * SEQ
NT = -(-BATCH // IMGS)
TOKENS = BATCH * SEQ
LAST = TOKENS - (NT - 1) * T
D = 256
DC = D // P
PD = 768
PC = PD // P
HEADS = 16
HD = D // HEADS
HPC = P // HD
HB = 4
E = 8
CAP = TOKENS // E
HID = 512
HC = HID // P
EPS = 1e-5
ROW = D + E

J = P // E
F = TOKENS // J
FH = F // 2
LO = 16
HI = -(-CAP // LO)
ST = 3
SP_ = -(-CAP // ST)
SEARCH = 15

C_ID = 0
C_MASK = C_ID + P
C_COS = C_MASK + T
C_SIN = C_COS + 2 * D
C_HEAD = C_SIN + 2 * D
C_E8 = C_HEAD + HPC
C_SCALE = C_E8 + E
C_FROW = C_SCALE + SEARCH
NC_F = C_FROW + 1
I_BITS = 0
I_HI = I_BITS + 3 * SEARCH
I_LO = I_HI + HI
I_U = I_LO + LO
I_BLOCK = I_U + 2 * P
I_TRI = I_BLOCK + P
NC_I = I_TRI + P

STAGES = 4
NW = 2
PEELED = STAGES + 3
UNROLL = 3


class Tile:

    def __init__(self, i, slot, q):
        self.i, self.slot, self.q = i, slot, q


def run_steps(eng, step):
    def fixed(s):
        step([Tile(s - d, (s - d) % UNROLL, (s - d) // UNROLL) if 0 <= s - d < NT else None
              for d in range(STAGES + 1)])

    assert (NT - PEELED) % UNROLL == 0
    for s in range(PEELED):
        fixed(s)
    with eng.Fori(0, (NT - PEELED) // UNROLL) as j:
        for k in range(UNROLL):
            tiles = []
            for d in range(STAGES + 1):
                c = PEELED + k - d
                tiles.append(Tile(UNROLL * j + c, c % UNROLL, j + c // UNROLL))
            step(tiles)
    for s in range(NT, NT + STAGES):
        fixed(s)


def vit_tower(nc, x, consts, consts_i, ln1, lin_w, lin_b, affine_w, base, pos, w_qkv, w_out, wg, w1, w3, w2, out):
    ctx = ExitStack()
    with ctx:
        def sb(name, shape, dt=F32):
            return ctx.enter_context(nc.sbuf_tensor(name, shape, dt))

        def sem(name):
            return ctx.enter_context(nc.semaphore(name))

        def sems(name, n):
            return [sem(f"{name}{k}") for k in range(n)]

        def slots(name, shape, dt=F32, n=UNROLL):
            return [sb(f"{name}{k}", shape, dt) for k in range(n)]

        rows_dram = nc.dram_tensor("token_rows", (NT * T, ROW), F32, kind="Internal").ap()
        scores_dram = nc.dram_tensor("token_scores", (E, TOKENS), F32, kind="Internal").ap()
        ids_dram = nc.dram_tensor("slot_ids", (E, HI * LO), U32, kind="Internal").ap()

        cf = sb("cf", [P, NC_F])
        ci = sb("ci", [P, NC_I], I32)
        ident = cf[:, C_ID:C_ID + P]
        causal = cf[0:T, C_MASK:C_MASK + T]
        cos_t = cf[0:T, C_COS:C_COS + 2 * D]
        sin_t = cf[0:T, C_SIN:C_SIN + 2 * D]
        head_of = cf[:, C_HEAD:C_HEAD + HPC]
        expert_of = cf[:, C_E8:C_E8 + E]
        ln1_sb = sb("ln1_sb", [P, 2, PC])
        lin_sb = sb("lin_sb", [P, PC, D])
        linb_sb = sb("linb_sb", [1, D])
        bias_cols = sb("bias_cols", [P, PC, T])
        bias_sb = sb("bias_sb", [T, D])
        affw_sb = sb("affw_sb", [T, D])
        base_sb = sb("base_sb", [T, D])
        pos_sb = sb("pos_sb", [T, D])
        wqkv_sb = sb("wqkv_sb", [P, DC, 3 * D])
        wout_sb = sb("wout_sb", [P, DC, D])
        wg_sb = sb("wg_sb", [P, DC, E])
        ones = sb("ones", [P, P])
        neg_half = sb("neg_half", [P, 1])

        scores = sb("scores", [E, NT * T])
        w1_sb = slots("w1_sb", [P, DC, HID], n=NW)
        w3_sb = slots("w3_sb", [P, DC, HID], n=NW)
        w2_sb = slots("w2_sb", [P, HC, D], n=NW)

        lasting = ctx
        ctx = lasting.enter_context(ExitStack())
        x_in = slots("x_in", [T, PD])
        x_t = slots("x_t", [P, PC, T])
        y = slots("y", [T, D])
        h = slots("h", [T, D])
        xa = slots("xa", [T, D])
        xa_t = slots("xa_t", [P, DC, T])
        qk = slots("qk", [T, 2 * D])
        v1 = slots("v1", [T, HEADS, HD + 1])
        rope_a = sb("rope_a", [T, 2 * D])
        rope_b = sb("rope_b", [T, 2 * D])
        qkr = slots("qkr", [T, 2 * D])
        neg = slots("neg", [T, 2 * D])
        feat = slots("feat", [T, 2 * D])
        qk_t = slots("qk_t", [P, 2 * DC, T])
        q_masked = sb("q_masked", [P, DC, HPC, T])
        s_t = slots("s_t", [T, HEADS, T])
        den = slots("den", [T, 2, HEADS])
        att = slots("att", [T, D])
        att_t = slots("att_t", [P, DC, T])
        h2 = slots("h2", [T, D])
        row = slots("row", [T, ROW])
        x2_t = slots("x2_t", [P, DC, T])
        stat = {n: slots(f"stat_{n}", [T, 12]) for n in ("ln1", "ln2", "ln3", "ln4")}
        mean_var = {n: slots(f"mv_{n}", [T, 2]) for n in ("ln1", "ln2", "ln3", "ln4")}
        var_eps = {n: slots(f"ve_{n}", [T, 1]) for n in ("ln1", "ln2", "ln3", "ln4")}
        rstd = {n: slots(f"rstd_{n}", [T, 1]) for n in ("ln1", "ln2", "ln3", "ln4")}

        ctx.close()
        ctx = lasting

        bank = [ctx.enter_context(nc.psum_tensor(f"bank{k}", [P, 512], F32)) for k in range(8)]
        S_BANKS = bank[0:4]
        B4, B5, B6, B7 = bank[4:8]

        const_loaded = sem("const_loaded")
        setup = sem("setup")
        bias_summed = sem("bias_summed")
        pool_ready = sem("pool_ready")
        x_loaded = sems("x_loaded", UNROLL)
        h2_stored = sems("h2_stored", UNROLL)
        row_stored = sems("row_stored", UNROLL)
        LN_STEPS = 4
        ln = {n: sem(f"dve_{n}") for n in ("ln1", "ln2", "ln3", "ln4")}
        rs = {n: sem(f"pool_{n}") for n in ("ln1", "ln2", "ln3", "ln4")}
        biased = sem("biased")
        affined = sem("affined")
        roped = sem("roped")
        rectified = sem("rectified")
        feat_ready = sem("feat_ready")
        q_ready = sem("q_ready")
        s_masked = sem("s_masked")
        att_steps = sem("att_steps")
        h2_ready = sem("h2_ready")
        sc_copied = sem("sc_copied")
        pe_xt, pe_y, pe_xat, pe_qk, pe_v, pe_qkt, pe_s, pe_av, pe_at, pe_o, pe_x2t, pe_sc, pe_sct = (
            sem(n) for n in ("pe_xt", "pe_y", "pe_xat", "pe_qk", "pe_v", "pe_qkt", "pe_s", "pe_av", "pe_at",
                             "pe_o", "pe_x2t", "pe_sc", "pe_sct"))
        a_xt, a_xat, a_qk, a_v, a_qkt, a_at, a_x2t, a_sct = (
            sem(n) for n in ("a_xt", "a_xat", "a_qk", "a_v", "a_qkt", "a_at", "a_x2t", "a_sct"))
        N_CONST = 13

        w_loaded = sems("w_loaded", NW)
        sc128 = sb("sc128", [P, F])
        yv = sb("yv", [P, F])
        junk = sb("junk", [P, F])
        below = sb("below", [P, 3, F])
        sel_gt = sb("sel_gt", [P, F])
        sel_eq = sb("sel_eq", [P, F])
        scan = sb("scan", [P, F])
        picked = sb("picked", [P, F])
        ex = sb("ex", [P, F])
        zeros = sb("zeros", [P, F])
        cnt = sb("cnt", [P, 8], BF16)
        col = sb("col", [P, 16])
        t_int = sb("t_int", [P, 1], I32)
        a_int = sb("a_int", [P, 1], I32)
        cand = sb("cand", [P, 3], I32)
        junk3 = sb("junk3", [P, 3])
        block_ones = sb("block_ones", [P, P], BF16)
        block_tri = sb("block_tri", [P, P], BF16)
        diag_max = sb("diag_max", [P, P])
        max8 = sb("max8", [P, E])
        neg_max8 = sb("neg_max8", [P, E])
        e8 = sb("e8", [P, E])
        rz8 = sb("rz8", [P, E])
        slot_t = sb("slot_t", [FH, 2 * P], I32)
        hi_t = sb("hi_t", [FH, 2 * P], I32)
        lo_t = sb("lo_t", [FH, 2 * P], I32)
        hot_hi = sb("hot_hi", [FH, 2 * P, HI], BF16)
        hot_lo = sb("hot_lo", [FH, 2 * P, LO], BF16)
        hot_id = sb("hot_id", [FH, 2 * P, 2, LO], BF16)
        u_bf = sb("u_bf", [FH, 2 * P], BF16)
        id_f = sb("id_f", [HI, E, LO])
        id_u = sb("id_u", [HI, E, LO], U32)
        ids = sb("ids", [SP_, E, ST], U32)
        xg = slots("xg", [SP_, ST, ROW], n=2)
        xg_t = slots("xg_t", [P, DC, CAP], n=2)
        gate = slots("gate", [P, CAP], n=2)
        hid = slots("hid", [P, HC, CAP], n=2)
        w_slot = slots("w_slot", [SP_, ST, 2], n=2)
        y_w = slots("y_w", [SP_, ST, D], n=2)

        scores_out = sem("scores_out")
        scores_in = sem("scores_in")
        topk = sem("topk")
        pe_cnt = sem("pe_cnt")
        act_ex = sem("act_ex")
        pe_tk = sem("pe_tk")
        ids_out = sem("ids_out")
        ids_in = sem("ids_in")
        gathered = sems("gathered", 2)
        scattered = sem("scattered")
        pe_xgt = sem("pe_xgt")
        a_xgt = sem("a_xgt")
        pe_h = sem("pe_h")
        a_gate = sem("a_gate")
        hid_ready = sem("hid_ready")
        pe_y2 = sem("pe_y2")
        a_exp = sem("a_exp")
        w_ready = sem("w_ready")
        y_ready = sem("y_ready")

        def width(t):
            return LAST if isinstance(t.i, int) and t.i == NT - 1 else T

        def rows_of(dram, t, n):
            return dram[t.i * T:t.i * T + n, :] if isinstance(t.i, int) else dram[bass.ds(t.i * T, n), :]

        x_flat = x.rearrange("n t f -> (n t) f")
        out_flat = out.rearrange("b n d -> (b n) d")

        block = ctx.enter_context(nc.Block())

        @block.sync
        def _(sp):
            sp.dma_start(cf[:], consts).then_inc(const_loaded, 16)
            sp.dma_start(ci[:], consts_i).then_inc(const_loaded, 16)
            sp.dma_start(ln1_sb[:], ln1).then_inc(const_loaded, 16)
            sp.dma_start(lin_sb[:], lin_w.rearrange("(c p) d -> p c d", p=P)).then_inc(const_loaded, 16)
            sp.dma_start(linb_sb[:], lin_b).then_inc(const_loaded, 16)
            sp.dma_start(affw_sb[:], affine_w).then_inc(const_loaded, 16)
            sp.dma_start(base_sb[:], base).then_inc(const_loaded, 16)
            sp.dma_start(pos_sb[:], pos).then_inc(const_loaded, 16)
            sp.dma_start(wqkv_sb[:], w_qkv.rearrange("(c p) d -> p c d", p=P)).then_inc(const_loaded, 16)
            sp.dma_start(wout_sb[:], w_out.rearrange("(c p) d -> p c d", p=P)).then_inc(const_loaded, 16)
            sp.dma_start(wg_sb[:], wg.rearrange("(c p) e -> p c e", p=P)).then_inc(const_loaded, 16)

            def load_expert(e):
                w = e % NW
                sp.dma_start(w1_sb[w][:], w1[e].rearrange("(c p) h -> p c h", p=P)).then_inc(w_loaded[w], 16)
                sp.dma_start(w3_sb[w][:], w3[e].rearrange("(c p) h -> p c h", p=P)).then_inc(w_loaded[w], 16)
                sp.dma_start(w2_sb[w][:], w2[e].rearrange("(m p) d -> p m d", p=P)).then_inc(w_loaded[w], 16)

            def step(tiles):
                t = tiles[0]
                if t:
                    if not isinstance(t.i, int) or t.i >= UNROLL:
                        sp.wait_ge(pe_xt, t.i - (UNROLL - 1))
                    sp.dma_start(x_in[t.slot][:], rows_of(x_flat, t, T)).then_inc(x_loaded[t.slot], 16)
                t = tiles[4]
                if t:
                    n = width(t)
                    sp.wait_ge(h2_ready, t.i + 1)
                    sp.dma_start(rows_of(out_flat, t, n), h2[t.slot][0:n, :]).then_inc(h2_stored[t.slot], 16)
                    sp.wait_ge(sc_copied, t.i + 1)
                    sp.dma_start(rows_of(rows_dram, t, T), row[t.slot][:]).then_inc(row_stored[t.slot], 16)

            run_steps(sp, step)
            for e in range(NW):
                load_expert(e)
            sp.wait_ge(a_sct, NT)
            sp.dma_start(scores_dram, scores[:, 0:TOKENS]).then_inc(scores_out, 16)
            sp.wait_ge(scores_out, 16)
            sp.dma_start(sc128[:], scores_dram.rearrange("e (j f) -> (e j) f", j=J)).then_inc(scores_in, 16)
            sp.wait_ge(topk, TK_IDS)
            sp.dma_start(ids_dram.rearrange("e (hi lo) -> hi e lo", lo=LO), id_u[:]).then_inc(ids_out, 16)
            sp.wait_ge(ids_out, 16)
            sp.dma_start(ids[:], ids_dram[:, 0:SP_ * ST].rearrange("e (p s) -> p e s", s=ST)).then_inc(ids_in, 16)
            for e in range(NW, E):
                sp.wait_ge(pe_y2, ST * (e - NW + 1))
                load_expert(e)

        @block.tensor
        def _(pe):
            pe.wait_ge(setup, 2)
            for c in range(PC):
                pe.matmul(B7[0:T, 0:D], bias_cols[:, c, :], lin_sb[:, c, :], start=(c == 0), stop=False)
            pe.matmul(B7[0:T, 0:D], ones[0:1, 0:T], linb_sb[:], start=False, stop=True).then_inc(bias_summed, 1)

            def step(tiles):
                t1, t2, t3, t4 = tiles[1:5]
                if t1:
                    pe.wait_ge(ln["ln1"], LN_STEPS * t1.i + 4)
                    for c in range(PC):
                        o = B4[:, c * T:(c + 1) * T] if c < 4 else B5[:, (c - 4) * T:(c - 3) * T]
                        mm = pe.transpose(o, x_in[t1.slot][:, c * P:(c + 1) * P], ident[0:T, 0:T])
                    mm.then_inc(pe_xt, 1)
                if t3:
                    pe.wait_ge(s_masked, 4 * t3.i + 4)
                    pe.wait_ge(a_v, t1.i if t1 else NT)
                    if not t1:
                        pe.wait_ge(sc_copied, t3.i)
                    for n in range(HEADS):
                        mm = pe.matmul(B6[0:T, n * (HD + 1):(n + 1) * (HD + 1)], s_t[t3.slot][:, n, :],
                                       v1[t3.slot][:, n, :], start=True, stop=True)
                    mm.then_inc(pe_av, 1)
                if t1:
                    pe.wait_ge(a_xt, t1.i + 1)
                    if isinstance(t1.i, int) and t1.i == 0:
                        pe.wait_ge(setup, 4)
                    else:
                        pe.wait_ge(a_qk, t1.i)
                    for c in range(PC):
                        mm = pe.matmul(B7[0:T, 0:D], x_t[t1.slot][:, c, :], lin_sb[:, c, :],
                                       start=(c == 0), stop=(c == PC - 1))
                    mm.then_inc(pe_y, 1)
                if t3:
                    pe.wait_ge(att_steps, 3 * t3.i + 3)
                    if not t1:
                        pe.wait_ge(a_xt, NT)
                    for c in range(DC):
                        mm = pe.transpose(B4[:, c * T:(c + 1) * T], att[t3.slot][:, c * P:(c + 1) * P],
                                          ident[0:T, 0:T])
                    mm.then_inc(pe_at, 1)
                if t4:
                    pe.wait_ge(sc_copied, t4.i + 1)
                    if not t3:
                        pe.wait_ge(a_at, NT)
                    pe.transpose(B4[0:E, DC * T:(DC + 1) * T], row[t4.slot][:, D:ROW],
                                 ident[0:T, 0:T]).then_inc(pe_sct, 1)
                if t2:
                    pe.wait_ge(feat_ready, t2.i + 1)
                    if not t1:
                        pe.wait_ge(a_xat, NT)
                    for c in range(2 * DC):
                        mm = pe.transpose(B5[:, c * T:(c + 1) * T], feat[t2.slot][:, c * P:(c + 1) * P],
                                          ident[0:T, 0:T])
                    mm.then_inc(pe_qkt, 1)
                if t3:
                    pe.wait_ge(a_at, t3.i + 1)
                    for c in range(DC):
                        mm = pe.matmul(B6[0:T, 0:D], att_t[t3.slot][:, c, :], wout_sb[:, c, :],
                                       start=(c == 0), stop=(c == DC - 1))
                    mm.then_inc(pe_o, 1)
                if t2:
                    pe.wait_ge(q_ready, t2.i + 1)
                    for b in range(4):
                        c, g = b // 2, b % 2
                        pe.matmul(S_BANKS[b][0:T, 0:HB * T], qk_t[t2.slot][:, DC + c, :],
                                  q_masked[:, c, g * HB:(g + 1) * HB, :], start=True, stop=True).then_inc(pe_s, 1)
                if t3:
                    pe.wait_ge(ln["ln4"], LN_STEPS * t3.i + 4)
                    if t4:
                        pe.wait_ge(a_sct, t4.i + 1)
                    for c in range(DC):
                        mm = pe.transpose(B4[:, c * T:(c + 1) * T], row[t3.slot][:, c * P:(c + 1) * P],
                                          ident[0:T, 0:T])
                    mm.then_inc(pe_x2t, 1)
                if t1:
                    pe.wait_ge(ln["ln3"], LN_STEPS * t1.i + 4)
                    if t2:
                        pe.wait_ge(a_qkt, t2.i + 1)
                    for c in range(DC):
                        mm = pe.transpose(B5[:, c * T:(c + 1) * T], xa[t1.slot][:, c * P:(c + 1) * P],
                                          ident[0:T, 0:T])
                    mm.then_inc(pe_xat, 1)
                if t3:
                    pe.wait_ge(a_x2t, t3.i + 1)
                    for c in range(DC):
                        mm = pe.matmul(B6[0:T, 0:E], x2_t[t3.slot][:, c, :], wg_sb[:, c, :],
                                       start=(c == 0), stop=(c == DC - 1))
                    mm.then_inc(pe_sc, 1)
                if t1:
                    pe.wait_ge(a_xat, t1.i + 1)
                    for c in range(DC):
                        mm = pe.matmul(B7[0:T, 0:2 * D], xa_t[t1.slot][:, c, :], wqkv_sb[:, c, 0:2 * D],
                                       start=(c == 0), stop=(c == DC - 1))
                    mm.then_inc(pe_qk, 1)
                    if t3:
                        pe.wait_ge(sc_copied, t3.i + 1)
                    for c in range(DC):
                        mm = pe.matmul(B6[0:T, 0:D], xa_t[t1.slot][:, c, :], wqkv_sb[:, c, 2 * D:3 * D],
                                       start=(c == 0), stop=(c == DC - 1))
                    mm.then_inc(pe_v, 1)

            run_steps(pe, step)

            def count(n, lhs, rhs, o, dve_at):
                pe.wait_ge(topk, dve_at)
                pe.matmul(o, lhs, rhs, start=True, stop=True).then_inc(pe_cnt, 1)

            pe.wait_ge(sc_copied, NT)
            pe.wait_ge(a_qkt, NT)
            pe.wait_ge(a_sct, NT)
            count(0, block_ones[:], cnt[:, 0:1], B7[:, 0:1], TK_SIGN)
            count(1, ones[:], diag_max[:], B6[:, 0:P], TK_MAX)
            with pe.Fori(0, SEARCH) as r:
                pe.wait_ge(topk, TK_SEARCH + TK_ROUND * r + 2)
                pe.matmul(B7[:, 0:3], block_ones[:], cnt[:, 1:4], start=True, stop=True).then_inc(pe_cnt, 1)
            count(0, block_ones[:], cnt[:, 1:2], B7[:, 0:1], TK_LAST + 2)
            pe.wait_ge(topk, TK_GT)
            pe.matmul(B7[:, 0:1], block_ones[:], cnt[:, 4:5], start=True, stop=True)
            pe.matmul(B7[:, 1:2], block_tri[:], cnt[:, 5:6], start=True, stop=True).then_inc(pe_cnt, 1)
            count(0, block_tri[:], cnt[:, 6:7], B7[:, 0:1], TK_SEL)
            pe.wait_ge(topk, TK_Z)
            pe.matmul(B6[:, 0:E], ones[:], e8[:], start=True, stop=True).then_inc(pe_cnt, 1)
            pe.wait_ge(topk, TK_POS)
            for c in range(2):
                mm = pe.transpose(B4[0:FH, c * P:(c + 1) * P], picked[:, c * FH:(c + 1) * FH], ident)
            mm.then_inc(pe_cnt, 1)
            pe.wait_ge(topk, TK_HOT)
            for e in range(E):
                for n in range(2 * J):
                    k = (n // J) * P + e * J + n % J
                    mm = pe.matmul(B5[0:HI, e * 2 * LO:(e + 1) * 2 * LO], hot_hi[:, k, :],
                                   hot_id[:, k, :, :], start=(n == 0), stop=(n == 2 * J - 1))
            mm.then_inc(pe_cnt, 1)

            def up(e):
                pe.wait_ge(gathered[e % 2], 16 * ST * (e // 2 + 1))
                if e >= 1:
                    pe.wait_ge(a_xgt, 2 * e)
                for c in range(DC):
                    for s in range(ST):
                        n = min(SP_, CAP - s * SP_)
                        mm = pe.transpose(bank[c][:, s * SP_:s * SP_ + n], xg[e % 2][0:n, s, c * P:(c + 1) * P],
                                          ident[0:n, 0:n])
                    mm.then_inc(pe_xgt, 1)

            def hidden(e):
                pe.wait_ge(w_loaded[e % NW], 48 * (e // NW + 1))
                pe.wait_ge(a_xgt, 2 * (e + 1))
                for m in range(HC):
                    k = HC * e + m
                    if k >= 2:
                        pe.wait_ge(hid_ready, k - 1)
                    g, u = bank[2 + 2 * (k % 2)], bank[3 + 2 * (k % 2)]
                    for c in range(DC):
                        pe.matmul(g[:, 0:CAP], w1_sb[e % NW][:, c, m * P:(m + 1) * P], xg_t[e % 2][:, c, :],
                                  start=(c == 0), stop=(c == DC - 1))
                    for c in range(DC):
                        mm = pe.matmul(u[:, 0:CAP], w3_sb[e % NW][:, c, m * P:(m + 1) * P], xg_t[e % 2][:, c, :],
                                       start=(c == 0), stop=(c == DC - 1))
                    mm.then_inc(pe_h, 1)

            def down(e):
                pe.wait_ge(hid_ready, HC * (e + 1))
                for s in range(ST):
                    n = min(SP_, CAP - s * SP_)
                    k = ST * e + s
                    if k >= 2:
                        pe.wait_ge(y_ready, k - 1)
                    for m in range(HC):
                        mm = pe.matmul(bank[6 + k % 2][0:n, 0:D], hid[e % 2][:, m, s * SP_:s * SP_ + n],
                                       w2_sb[e % NW][:, m, :], start=(m == 0), stop=(m == HC - 1))
                    mm.then_inc(pe_y2, 1)

            pe.wait_ge(topk, TK_IDS)
            up(0)
            for e in range(E):
                hidden(e)
                if e + 1 < E:
                    up(e + 1)
                down(e)

        @block.scalar
        def _(act):
            def step(tiles):
                t1, t2, t3, t4 = tiles[1:5]
                if t1:
                    act.wait_ge(pe_xt, t1.i + 1)
                    nc.scalar.copy(x_t[t1.slot][:, 0:4, :], B4[:, 0:4 * T])
                    nc.scalar.copy(x_t[t1.slot][:, 4:PC, :], B5[:, 0:(PC - 4) * T]).then_inc(a_xt, 1)
                if t2:
                    act.wait_ge(roped, 4 * t2.i + 4)
                    nc.scalar.activation(neg[t2.slot][:], qkr[t2.slot][:], ACT.Relu, scale=-1.0).then_inc(rectified, 1)
                    act.wait_ge(rectified, 2 * t2.i + 1)
                    nc.scalar.activation(neg[t2.slot][:], neg[t2.slot][:], ACT.Exp, scale=-1.0).then_inc(rectified, 1)
                if t3:
                    act.wait_ge(pe_at, t3.i + 1)
                    if t4:
                        act.wait_ge(pe_sct, t4.i + 1)
                    nc.scalar.copy(att_t[t3.slot][:], B4[:, 0:DC * T]).then_inc(a_at, 1)
                if t4:
                    act.wait_ge(pe_sct, t4.i + 1)
                    o = (scores[:, t4.i * T:(t4.i + 1) * T] if isinstance(t4.i, int)
                         else scores[:, bass.ds(t4.i * T, T)])
                    nc.scalar.copy(o, B4[0:E, DC * T:(DC + 1) * T]).then_inc(a_sct, 1)
                if t2:
                    act.wait_ge(pe_qkt, t2.i + 1)
                    nc.scalar.copy(qk_t[t2.slot][:], B5[:, 0:2 * DC * T]).then_inc(a_qkt, 1)
                if t3:
                    act.wait_ge(pe_x2t, t3.i + 1)
                    nc.scalar.copy(x2_t[t3.slot][:], B4[:, 0:DC * T]).then_inc(a_x2t, 1)
                if t1:
                    act.wait_ge(pe_xat, t1.i + 1)
                    nc.scalar.copy(xa_t[t1.slot][:], B5[:, 0:DC * T]).then_inc(a_xat, 1)
                    act.wait_ge(pe_qk, t1.i + 1)
                    nc.scalar.copy(qk[t1.slot][:], B7[0:T, 0:2 * D]).then_inc(a_qk, 1)
                    act.wait_ge(pe_v, t1.i + 1)
                    nc.scalar.copy(v1[t1.slot][:, :, 0:HD],
                                   B6[0:T, 0:D].rearrange("t (n d) -> t n d", n=HEADS)).then_inc(a_v, 1)

            act.wait_ge(setup, 4)
            run_steps(act, step)

            act.wait_ge(topk, TK_MAXOWN)
            nc.scalar.activation(ex[:], sc128[:], ACT.Exp, bias=col[:, 5:6]).then_inc(act_ex, 1)

            for e in range(E):
                act.wait_ge(gathered[e % 2], 16 * ST * (e // 2 + 1))
                if e == 0:
                    act.wait_ge(topk, TK_IDS)
                if e >= 2:
                    act.wait_ge(y_ready, ST * (e - 1))
                for s in range(ST):
                    n = min(SP_, CAP - s * SP_)
                    last = nc.scalar.activation(w_slot[e % 2][0:n, s, 0:1], xg[e % 2][0:n, s, D + e:D + e + 1],
                                                ACT.Exp, bias=neg_max8[0:n, e:e + 1])
                last.then_inc(a_exp, 1)
                for c in range(DC):
                    act.wait_ge(pe_xgt, 2 * e + c + 1)
                    nc.scalar.copy(xg_t[e % 2][:, c, :], bank[c][:, 0:CAP]).then_inc(a_xgt, 1)
                for m in range(HC):
                    k = HC * e + m
                    act.wait_ge(pe_h, k + 1)
                    if k >= 2:
                        act.wait_ge(hid_ready, k - 1)
                    nc.scalar.activation(gate[k % 2][:], bank[2 + 2 * (k % 2)][:, 0:CAP], ACT.Silu).then_inc(a_gate, 1)

        @block.vector
        def _(dve):
            V = nc.vector
            n_setup = [0]

            def setup_step(ins):
                n_setup[0] += 1
                ins.then_inc(setup, 1)

            V.memset(ones[:], 1.0)
            for k in range(UNROLL):
                V.memset(v1[k][:], 1.0)
            setup_step(V.memset(neg_half[:], -0.5))
            dve.wait_ge(setup, 1)
            dve.wait_ge(const_loaded, 16 * 11)
            for c in range(PC):
                last = V.tensor_scalar(bias_cols[:, c, :], ones[:, 0:T], ln1_sb[:, 1, c:c + 1], None, ALU.mult)
            setup_step(last)
            V.tensor_tensor(base_sb[:], base_sb[:], pos_sb[:], ALU.add)
            dve.wait_ge(bias_summed, 1)
            V.tensor_copy(bias_sb[:], B7[0:T, 0:D]).then_inc(setup, 1)
            for c in range(PC):
                last = V.tensor_scalar(lin_sb[:, c, :], lin_sb[:, c, :], ln1_sb[:, 0, c:c + 1], None, ALU.mult)
            last.then_inc(setup, 1)
            dve.wait_ge(setup, 4)

            def ln_stats(n, t, src, width):
                parts = -(-width // 512)
                w = width // parts
                for k in range(parts):
                    last = V.bn_stats(stat[n][t.slot][:, 6 * k:6 * k + 6], src[:, k * w:(k + 1) * w])
                last.then_inc(ln[n], 1)
                dve.wait_ge(ln[n], LN_STEPS * t.i + 1)
                V.memset(var_eps[n][t.slot][:], EPS)
                V.bn_aggr(mean_var[n][t.slot][:], stat[n][t.slot][:, 0:6 * parts]).then_inc(ln[n], 1)
                dve.wait_ge(ln[n], LN_STEPS * t.i + 2)
                V.tensor_tensor(var_eps[n][t.slot][:], var_eps[n][t.slot][:], mean_var[n][t.slot][:, 1:2],
                                ALU.add).then_inc(ln[n], 1)

            def ln_scale(n, t, dst, src):
                dve.wait_ge(rs[n], t.i + 1)
                V.tensor_scalar(dst, src, mean_var[n][t.slot][:, 0:1], rstd[n][t.slot][:], ALU.subtract,
                                ALU.mult).then_inc(ln[n], 1)

            def step(tiles):
                t0, t1, t2, t3, t4 = tiles
                if t3:
                    dve.wait_ge(pe_av, t3.i + 1)
                    o = B6[0:T, 0:HEADS * (HD + 1)].rearrange("t (n d) -> t n d", n=HEADS)
                    V.tensor_scalar(den[t3.slot][:, 0, :], o[:, :, HD], 1e-6, None, ALU.max).then_inc(att_steps, 1)
                    dve.wait_ge(att_steps, 3 * t3.i + 1)
                    V.reciprocal(den[t3.slot][:, 1, :], den[t3.slot][:, 0, :]).then_inc(att_steps, 1)
                    dve.wait_ge(att_steps, 3 * t3.i + 2)
                    V.tensor_tensor(att[t3.slot][:].rearrange("t (n d) -> t n d", n=HEADS), o[:, :, 0:HD],
                                    den[t3.slot][:, 1, :].unsqueeze(2).broadcast_to([T, HEADS, HD]),
                                    ALU.mult).then_inc(att_steps, 1)
                if t2:
                    dve.wait_ge(rectified, 2 * t2.i + 2)
                    V.scalar_tensor_tensor(out=feat[t2.slot][:], in0=qkr[t2.slot][:], scalar=0.0,
                                           in1=neg[t2.slot][:], op0=ALU.max, op1=ALU.add).then_inc(feat_ready, 1)
                if t1:
                    dve.wait_ge(pe_y, t1.i + 1)
                    V.tensor_tensor(y[t1.slot][:], B7[0:T, 0:D], bias_sb[:], ALU.add).then_inc(biased, 1)
                    dve.wait_ge(biased, t1.i + 1)
                    ln_stats("ln2", t1, y[t1.slot], D)
                if t2:
                    dve.wait_ge(a_qkt, t2.i + 1)
                    for c in range(DC):
                        last = V.tensor_tensor(q_masked[:, c, :, :],
                                               qk_t[t2.slot][:, c, :].unsqueeze(1).broadcast_to([P, HPC, T]),
                                               head_of.unsqueeze(2).broadcast_to([P, HPC, T]), ALU.mult)
                    last.then_inc(q_ready, 1)
                if t1:
                    ln_scale("ln2", t1, y[t1.slot][:], y[t1.slot][:])
                if t3:
                    dve.wait_ge(pe_o, t3.i + 1)
                    if not isinstance(t3.i, int) or t3.i >= UNROLL:
                        dve.wait_ge(h2_stored[t3.slot], 16 * t3.q)
                        dve.wait_ge(row_stored[t3.slot], 16 * t3.q)
                    V.tensor_tensor(h2[t3.slot][:], B6[0:T, 0:D], h[t3.slot][:], ALU.add).then_inc(h2_ready, 1)
                    dve.wait_ge(h2_ready, t3.i + 1)
                    ln_stats("ln4", t3, h2[t3.slot], D)
                if t1:
                    dve.wait_ge(affined, 2 * t1.i + 2)
                    ln_stats("ln3", t1, h[t1.slot], D)
                if t3:
                    ln_scale("ln4", t3, row[t3.slot][:, 0:D], h2[t3.slot][:])
                if t1:
                    ln_scale("ln3", t1, xa[t1.slot][:], h[t1.slot][:])
                if t2:
                    for b in range(4):
                        dve.wait_ge(pe_s, 4 * t2.i + b + 1)
                        V.tensor_tensor(s_t[t2.slot][:, b * HB:(b + 1) * HB, :],
                                        S_BANKS[b][0:T, 0:HB * T].rearrange("s (n t) -> s n t", n=HB),
                                        causal.unsqueeze(1).broadcast_to([T, HB, T]),
                                        ALU.mult).then_inc(s_masked, 1)
                if t3:
                    dve.wait_ge(pe_sc, t3.i + 1)
                    V.tensor_copy(row[t3.slot][:, D:ROW], B6[0:T, 0:E]).then_inc(sc_copied, 1)
                if t0:
                    dve.wait_ge(x_loaded[t0.slot], 16 * t0.q + 16)
                    ln_stats("ln1", t0, x_in[t0.slot], PD)
                    ln_scale("ln1", t0, x_in[t0.slot][:], x_in[t0.slot][:])

            run_steps(dve, step)

            at = [0]

            def link(ins):
                at[0] += 1
                ins.then_inc(topk, 1)
                dve.wait_ge(topk, at[0])

            def mark(name):
                assert at[0] == name, (at[0], name)

            sgn, lim, t_s, need, nmax_own, acc, zc, soff, eoff, g_tot = (col[:, k:k + 1] for k in (0, 1, 2, 3, 5, 6, 7, 8, 9, 10))
            for k in range(UNROLL):
                n = len(range(k, NT, UNROLL))
                dve.wait_ge(h2_stored[k], 16 * n)
                dve.wait_ge(row_stored[k], 16 * n)
            V.memset(zeros[:], 0.0)
            V.memset(t_int[:], 0)
            V.tensor_copy(block_ones[:], ci[:, I_BLOCK:I_BLOCK + P])
            V.tensor_copy(block_tri[:], ci[:, I_TRI:I_TRI + P])
            V.tensor_copy(u_bf[:], ci[0:FH, I_U:I_U + 2 * P])
            dve.wait_ge(scores_in, 16)
            link(V.tensor_scalar(junk[:], sc128[:], 0.0, None, ALU.is_ge, ALU.add, accum_out=cnt[:, 0:1]))
            mark(TK_SIGN)
            link(V.reduce_max(acc, sc128[:], AX.X))
            link(V.tensor_scalar(diag_max[:], ident, acc, None, ALU.mult))
            mark(TK_MAX)
            dve.wait_ge(pe_cnt, 1)
            link(V.tensor_scalar(lim, B7[:, 0:1], float(CAP), 2.0, ALU.is_ge, ALU.mult))
            link(V.tensor_scalar(sgn, lim, -1.0, None, ALU.add))
            link(V.tensor_scalar(lim, sgn, (TOKENS - 2 * CAP + 1) / 2, (TOKENS - 1) / 2, ALU.mult, ALU.add))
            link(V.tensor_scalar(yv[:], sc128[:], sgn, None, ALU.mult))
            dve.wait_ge(pe_cnt, 2)
            link(V.reduce_max(max8[:], B6[:, 0:P].rearrange("p (e j) -> p e j", e=E), AX.X))
            link(V.tensor_scalar(neg_max8[:], max8[:], -1.0, None, ALU.mult))
            link(V.tensor_tensor(e8[:], neg_max8[:], expert_of, ALU.mult))
            link(V.reduce_sum(nmax_own, e8[:], AX.X))
            mark(TK_MAXOWN)
            mark(TK_SEARCH)

            def search(tab, scale, n, k, pe_k):
                V.tensor_tensor(cand[:, 0:n], t_int[:].broadcast_to([P, n]), tab, ALU.bitwise_or).then_inc(topk, 1)
                dve.wait_ge(topk, k + 1)
                for c in range(n):
                    last = V.tensor_scalar(below[:, c, :], yv[:], cand[:, c:c + 1].bitcast(F32), None, ALU.is_lt,
                                           ALU.add, accum_out=cnt[:, 1 + c:2 + c])
                last.then_inc(topk, 1)
                dve.wait_ge(pe_cnt, pe_k)
                V.tensor_scalar(junk3[:, 0:n], B7[:, 0:n], lim, None, ALU.is_le, ALU.add,
                                accum_out=acc).then_inc(topk, 1)
                dve.wait_ge(topk, k + 3)
                V.tensor_scalar(a_int[:], acc, scale, None, ALU.mult).then_inc(topk, 1)
                dve.wait_ge(topk, k + 4)
                V.tensor_tensor(t_int[:], t_int[:], a_int[:], ALU.bitwise_or).then_inc(topk, 1)
                dve.wait_ge(topk, k + 5)

            with dve.Fori(0, SEARCH) as r:
                search(ci[:, bass.ds(3 * r + I_BITS, 3)], cf[:, bass.ds(r + C_SCALE, 1)], 3,
                       TK_ROUND * r + TK_SEARCH, r + 3)
            search(ci[:, I_BITS:I_BITS + 1] if False else ci[:, I_LO + 1:I_LO + 2], 1.0, 1, TK_LAST, 3 + SEARCH)
            at[0] = TK_LAST + TK_ROUND
            n_pe = 3 + SEARCH
            link(V.tensor_scalar(t_s, t_int[:].bitcast(F32), sgn, None, ALU.mult))
            V.tensor_scalar(sel_gt[:], sc128[:], t_s, None, ALU.is_gt, ALU.add, accum_out=cnt[:, 4:5])
            link(V.tensor_scalar(sel_eq[:], sc128[:], t_s, None, ALU.is_equal, ALU.add, accum_out=cnt[:, 5:6]))
            mark(TK_GT)
            dve.wait_ge(pe_cnt, n_pe + 1)
            V.tensor_copy(eoff, B7[:, 1:2])
            link(V.tensor_scalar(need, B7[:, 0:1], -1.0, float(CAP), ALU.mult, ALU.add))
            link(V.tensor_tensor_scan(scan[:], sel_eq[:], zeros[:], eoff, ALU.add, ALU.add))
            link(V.scalar_tensor_tensor(out=junk[:], in0=scan[:], scalar=need, in1=sel_eq[:], op0=ALU.is_le,
                                        op1=ALU.mult))
            link(V.scalar_tensor_tensor(out=picked[:], in0=junk[:], scalar=0.0, in1=sel_gt[:], op0=ALU.add,
                                        op1=ALU.add, accum_out=cnt[:, 6:7]))
            mark(TK_SEL)
            dve.wait_ge(act_ex, 1)
            link(V.scalar_tensor_tensor(out=junk[:], in0=ex[:], scalar=1.0, in1=picked[:], op0=ALU.mult,
                                        op1=ALU.mult, accum_out=zc))
            link(V.tensor_scalar(e8[:], expert_of, zc, None, ALU.mult))
            mark(TK_Z)
            dve.wait_ge(pe_cnt, n_pe + 2)
            link(V.tensor_copy(soff, B7[:, 0:1]))
            link(V.tensor_tensor_scan(scan[:], picked[:], zeros[:], soff, ALU.add, ALU.add))
            link(V.tensor_tensor(picked[:], picked[:], scan[:], ALU.mult))
            mark(TK_POS)
            dve.wait_ge(pe_cnt, n_pe + 3)
            link(V.reciprocal(rz8[:], B6[:, 0:E]))
            dve.wait_ge(pe_cnt, n_pe + 4)
            link(V.tensor_scalar(slot_t[:], B4[0:FH, 0:2 * P], -1.0, None, ALU.add))
            link(V.tensor_scalar(hi_t[:], slot_t[:], 4, None, ALU.arith_shift_right))
            link(V.tensor_scalar(lo_t[:], slot_t[:], LO - 1, None, ALU.bitwise_and))
            V.tensor_tensor(hot_hi[:], hi_t[:].unsqueeze(2).broadcast_to([FH, 2 * P, HI]),
                            ci[0:FH, I_HI:I_HI + HI].unsqueeze(1).broadcast_to([FH, 2 * P, HI]), ALU.is_equal)
            link(V.tensor_tensor(hot_lo[:], lo_t[:].unsqueeze(2).broadcast_to([FH, 2 * P, LO]),
                                 ci[0:FH, I_LO:I_LO + LO].unsqueeze(1).broadcast_to([FH, 2 * P, LO]), ALU.is_equal))
            V.tensor_scalar(hot_id[:, :, 0, :], hot_lo[:], cf[0:FH, C_FROW:C_FROW + 1], None, ALU.mult)
            link(V.tensor_tensor(hot_id[:, :, 1, :], hot_lo[:],
                                 u_bf[:].unsqueeze(2).broadcast_to([FH, 2 * P, LO]), ALU.mult))
            mark(TK_HOT)
            dve.wait_ge(pe_cnt, n_pe + 5)
            o = B5[0:HI, 0:E * 2 * LO].rearrange("h (e k l) -> h e k l", e=E, k=2)
            link(V.tensor_copy(id_f[:], o[:, :, 0, :]))
            link(V.scalar_tensor_tensor(out=id_u[:], in0=o[:, :, 1, :], scalar=float(FH), in1=id_f[:],
                                        op0=ALU.mult, op1=ALU.add))
            mark(TK_IDS)

            for e in range(E):
                for m in range(HC):
                    k = HC * e + m
                    dve.wait_ge(a_gate, k + 1)
                    if m == 0 and e >= 2:
                        dve.wait_ge(pe_y2, ST * (e - 1))
                    V.tensor_tensor(hid[e % 2][:, m, :], gate[k % 2][:], bank[3 + 2 * (k % 2)][:, 0:CAP],
                                    ALU.mult).then_inc(hid_ready, 1)
                dve.wait_ge(a_exp, e + 1)
                if e >= 2:
                    dve.wait_ge(scattered, 16 * ST * (e - 1))
                V.tensor_scalar(w_slot[e % 2][:, 0:2, 1], w_slot[e % 2][:, 0:2, 0], rz8[0:SP_, e:e + 1], None, ALU.mult)
                n = CAP - 2 * SP_
                V.tensor_scalar(w_slot[e % 2][0:n, 2:3, 1], w_slot[e % 2][0:n, 2:3, 0], rz8[0:n, e:e + 1], None,
                                ALU.mult).then_inc(w_ready, 1)
                dve.wait_ge(w_ready, e + 1)
                for s in range(ST):
                    n = min(SP_, CAP - s * SP_)
                    k = ST * e + s
                    dve.wait_ge(pe_y2, k + 1)
                    V.tensor_scalar(y_w[e % 2][0:n, s, :], bank[6 + k % 2][0:n, 0:D], w_slot[e % 2][0:n, s, 1:2],
                                    None, ALU.mult).then_inc(y_ready, 1)

        @block.gpsimd
        def _(pool):
            G = nc.gpsimd

            def power(n, t):
                pool.wait_ge(ln[n], LN_STEPS * t.i + 3)
                G.tensor_tensor(rstd[n][t.slot][:], var_eps[n][t.slot][:], neg_half[0:T, :], ALU.pow).then_inc(rs[n], 1)

            def halves(a):
                return a.rearrange("t (n two d) -> t n two d", two=2, d=HD // 2)

            def step(tiles):
                t0, t1, t2, t3, t4 = tiles
                if t2:
                    pool.wait_ge(a_qk, t2.i + 1)
                    if not isinstance(t2.i, int) or t2.i >= 1:
                        pool.wait_ge(roped, 4 * t2.i)
                    a, b, s = halves(qk[t2.slot][:]), halves(rope_b[:]), halves(sin_t)
                    G.tensor_tensor(rope_a[:], qk[t2.slot][:], cos_t, ALU.mult).then_inc(roped, 1)
                    G.tensor_tensor(b[:, :, 0, :], a[:, :, 1, :], s[:, :, 0, :], ALU.mult).then_inc(roped, 1)
                    G.tensor_tensor(b[:, :, 1, :], a[:, :, 0, :], s[:, :, 1, :], ALU.mult).then_inc(roped, 1)
                    pool.wait_ge(roped, 4 * t2.i + 3)
                    G.tensor_tensor(qkr[t2.slot][:], rope_a[:], rope_b[:], ALU.add).then_inc(roped, 1)
                if t1:
                    power("ln2", t1)
                    pool.wait_ge(ln["ln2"], LN_STEPS * t1.i + 4)
                    G.tensor_tensor(h[t1.slot][:], y[t1.slot][:], affw_sb[:], ALU.mult).then_inc(affined, 1)
                    pool.wait_ge(affined, 2 * t1.i + 1)
                    G.tensor_tensor(h[t1.slot][:], h[t1.slot][:], base_sb[:], ALU.add).then_inc(affined, 1)
                if t3:
                    power("ln4", t3)
                if t1:
                    power("ln3", t1)
                if t0:
                    power("ln1", t0)

            pool.wait_ge(setup, 4)
            run_steps(pool, step)

            def gather(e):
                if e >= 2:
                    pool.wait_ge(pe_xgt, 2 * (e - 1))
                    pool.wait_ge(a_exp, e - 1)
                for s in range(ST):
                    n = min(SP_, CAP - s * SP_)
                    G.indirect_dma_start(xg[e % 2][0:n, s, :], None, rows_dram,
                                         bass.IndirectOffsetOnAxis(ids[0:n, e, s:s + 1], 0)
                                         ).then_inc(gathered[e % 2], 16)

            def scatter(e):
                for s in range(ST):
                    n = min(SP_, CAP - s * SP_)
                    pool.wait_ge(y_ready, ST * e + s + 1)
                    if e >= 1 and s == 0:
                        pool.wait_ge(scattered, 16 * ST * e)
                    G.indirect_dma_start(out_flat, bass.IndirectOffsetOnAxis(ids[0:n, e, s:s + 1], 0),
                                         y_w[e % 2][0:n, s, :], None, compute_op=ALU.add).then_inc(scattered, 16)

            for k in range(UNROLL):
                n = len(range(k, NT, UNROLL))
                pool.wait_ge(h2_stored[k], 16 * n)
                pool.wait_ge(row_stored[k], 16 * n)
            pool.wait_ge(ids_in, 16)
            gather(0)
            gather(1)
            for e in range(E):
                scatter(e)
                if e + 2 < E:
                    gather(e + 2)
            pool.wait_ge(scattered, 16 * ST * E)


TK_SIGN = 1
TK_MAX = 3
TK_MAXOWN = 11
TK_SEARCH = 11
TK_ROUND = 5
TK_LAST = TK_SEARCH + TK_ROUND * SEARCH
TK_GT = TK_LAST + TK_ROUND + 2
TK_SEL = TK_GT + 4
TK_Z = TK_SEL + 2
TK_POS = TK_Z + 3
TK_HOT = TK_POS + 6
TK_IDS = TK_HOT + 2


def constants():
    import numpy as np

    f = np.zeros((P, NC_F), np.float32)
    i = np.zeros((P, NC_I), np.int32)
    f[:, C_ID:C_ID + P] = np.eye(P)
    r = np.arange(T)
    f[:T, C_MASK:C_MASK + T] = (r[:, None] // SEQ == r[None, :] // SEQ) & (r[:, None] <= r[None, :])
    half = HD // 2
    inv = (1.0 / np.float32(10000.0) ** (np.arange(half, dtype=np.float32) / np.float32(half))).astype(np.float32)
    ang = ((r % SEQ).astype(np.float32)[:, None] * inv[None, :]).astype(np.float32)
    scale = np.float32(HD ** -0.25)
    cos, sin = np.cos(ang) * scale, np.sin(ang) * scale
    f[:T, C_COS:C_COS + 2 * D] = np.tile(np.concatenate([cos, cos], 1), (1, 2 * HEADS))
    f[:T, C_SIN:C_SIN + 2 * D] = np.tile(np.concatenate([-sin, sin], 1), (1, 2 * HEADS))
    p = np.arange(P)
    f[:, C_HEAD:C_HEAD + HPC] = p[:, None] // HD == np.arange(HPC)[None, :]
    f[:, C_E8:C_E8 + E] = p[:, None] // J == np.arange(E)[None, :]
    for n in range(SEARCH):
        shift = 2 * (SEARCH - n) - 1
        f[:, C_SCALE + n] = 2.0 ** shift
        i[:, I_BITS + 3 * n:I_BITS + 3 * n + 3] = np.array([1, 2, 3]) << shift
    f[:, C_FROW] = p
    i[:, I_HI:I_HI + HI] = np.arange(HI)
    i[:, I_LO:I_LO + LO] = np.arange(LO)
    k = np.arange(2 * P)
    i[:, I_U:I_U + 2 * P] = 2 * (k % J) + k // P
    same = p[:, None] // J == p[None, :] // J
    i[:, I_BLOCK:I_BLOCK + P] = same
    i[:, I_TRI:I_TRI + P] = same & (p[:, None] < p[None, :])
    return f, i


def kernel(**inputs):
    import numpy as np
    import concourse.bacc as bacc
    from concourse.bass_utils import run_bass_kernel_spmd

    x = np.asarray(inputs["x"])
    n_img, chans, height, wide = x.shape
    side = 16
    rows = np.zeros((NT * IMGS, SEQ, PD), x.dtype)
    rows[:n_img, 1:] = x.reshape(n_img, chans, height // side, side, wide // side, side).transpose(
        0, 2, 4, 3, 5, 1).reshape(n_img, SEQ - 1, PD)
    ln2_w, ln2_b = np.asarray(inputs["L0_tok_ln2_w"]), np.asarray(inputs["L0_tok_ln2_b"])
    affine_w = np.zeros((IMGS, SEQ, D), ln2_w.dtype)
    affine_w[:, 1:] = ln2_w
    base = np.zeros((IMGS, SEQ, D), ln2_b.dtype)
    base[:, 1:] = ln2_b
    base[:, 0] = np.asarray(inputs["L0_tok_cls_token"])[0, 0]
    pos = np.tile(np.asarray(inputs["L0_tok_pos_embedding"])[0, :SEQ], (IMGS, 1))
    cf, ci = constants()
    data = {
        "x": rows.reshape(NT, T, PD),
        "consts": cf,
        "consts_i": ci,
        "ln1": np.stack([np.asarray(inputs["L0_tok_ln1_w"]), np.asarray(inputs["L0_tok_ln1_b"])]
                        ).reshape(2, PC, P).transpose(2, 0, 1),
        "lin_w": np.asarray(inputs["L0_tok_lin_w"]),
        "lin_b": np.asarray(inputs["L0_tok_lin_b"]).reshape(1, D),
        "affine_w": affine_w.reshape(T, D),
        "base": base.reshape(T, D),
        "pos": pos,
        "w_qkv": np.asarray(inputs["L0_attn_w_qkv"]),
        "w_out": np.asarray(inputs["L0_attn_w_out"]),
        "wg": np.asarray(inputs["L0_ffn_Wg"]).T,
        "w1": np.asarray(inputs["L0_ffn_W1"]).transpose(0, 2, 1),
        "w3": np.asarray(inputs["L0_ffn_W3"]).transpose(0, 2, 1),
        "w2": np.asarray(inputs["L0_ffn_W2"]).transpose(0, 2, 1),
    }
    nc = bacc.Bacc("TRN2", target_bir_lowering=False, num_devices=1)
    arrays, args = {}, []
    for name, a in data.items():
        a = np.ascontiguousarray(a)
        arrays[f"in_{name}"] = a
        args.append(nc.dram_tensor(f"in_{name}", a.shape, mybir.dt.from_np(a.dtype), kind="ExternalInput").ap())
    out = nc.dram_tensor("out", (BATCH, SEQ, D), F32, kind="ExternalOutput").ap()
    vit_tower(nc, *args, out)
    r = run_bass_kernel_spmd(nc, [arrays], core_ids=[0])
    return r.results[0]["out"]
```

```python
from contextlib import ExitStack

import concourse.bass as bass
from concourse import mybir

F32 = mybir.dt.float32
BF16 = mybir.dt.bfloat16
I32 = mybir.dt.int32
U32 = mybir.dt.uint32
ALU = mybir.AluOpType
ACT = mybir.ActivationFunctionType
AX = mybir.AxisListType

P = 128
BATCH = 64
SEQ = 37
IMGS = 3
T = IMGS * SEQ
NT = -(-BATCH // IMGS)
TOKENS = BATCH * SEQ
LAST = TOKENS - (NT - 1) * T
D = 256
DC = D // P
PD = 768
PC = PD // P
HEADS = 16
HD = D // HEADS
HPC = P // HD
HB = 4
E = 8
CAP = TOKENS // E
HID = 512
HC = HID // P
EPS = 1e-5
ROW = D + E

J = P // E
F = TOKENS // J
FH = F // 2
LO = 16
HI = -(-CAP // LO)
ST = 3
SP_ = -(-CAP // ST)
SEARCH = 15

C_ID = 0
C_MASK = C_ID + P
C_COS = C_MASK + T
C_SIN = C_COS + 2 * D
C_HEAD = C_SIN + 2 * D
C_E8 = C_HEAD + HPC
C_SCALE = C_E8 + E
C_FROW = C_SCALE + SEARCH
NC_F = C_FROW + 1
I_BITS = 0
I_HI = I_BITS + 3 * SEARCH
I_LO = I_HI + HI
I_U = I_LO + LO
I_BLOCK = I_U + 2 * P
I_TRI = I_BLOCK + P
NC_I = I_TRI + P

AV_EARLY = 7
EARLY_HEADS = [range(k * AV_EARLY // (PC - 1), (k + 1) * AV_EARLY // (PC - 1)) for k in range(PC - 1)]
ROPE = 3
STAGES = 4
NW = 2
PEELED = STAGES + 3
UNROLL = 3


class Tile:

    def __init__(self, i, slot, q):
        self.i, self.slot, self.q = i, slot, q


def run_steps(eng, step):
    def fixed(s):
        step([Tile(s - d, (s - d) % UNROLL, (s - d) // UNROLL) if 0 <= s - d < NT else None
              for d in range(STAGES + 1)])

    assert (NT - PEELED) % UNROLL == 0
    for s in range(PEELED):
        fixed(s)
    with eng.Fori(0, (NT - PEELED) // UNROLL) as j:
        for k in range(UNROLL):
            tiles = []
            for d in range(STAGES + 1):
                c = PEELED + k - d
                tiles.append(Tile(UNROLL * j + c, c % UNROLL, j + c // UNROLL))
            step(tiles)
    for s in range(NT, NT + STAGES):
        fixed(s)


def vit_tower(nc, x, consts, consts_i, ln1, lin_w, lin_b, affine_w, base, pos, w_qkv, w_out, wg, w1, w3, w2, out):
    ctx = ExitStack()
    with ctx:
        def sb(name, shape, dt=F32):
            return ctx.enter_context(nc.sbuf_tensor(name, shape, dt))

        def sem(name):
            return ctx.enter_context(nc.semaphore(name))

        def sems(name, n):
            return [sem(f"{name}{k}") for k in range(n)]

        def slots(name, shape, dt=F32, n=UNROLL):
            return [sb(f"{name}{k}", shape, dt) for k in range(n)]

        rows_dram = nc.dram_tensor("token_rows", (NT * T, ROW), F32, kind="Internal").ap()
        scores_dram = nc.dram_tensor("token_scores", (E, TOKENS), F32, kind="Internal").ap()
        ids_dram = nc.dram_tensor("slot_ids", (E, HI * LO), U32, kind="Internal").ap()

        cf = sb("cf", [P, NC_F])
        ci = sb("ci", [P, NC_I], I32)
        ident = cf[:, C_ID:C_ID + P]
        causal = cf[0:T, C_MASK:C_MASK + T]
        cos_t = cf[0:T, C_COS:C_COS + 2 * D]
        sin_t = cf[0:T, C_SIN:C_SIN + 2 * D]
        head_of = cf[:, C_HEAD:C_HEAD + HPC]
        expert_of = cf[:, C_E8:C_E8 + E]
        ln1_sb = sb("ln1_sb", [P, 2, PC])
        lin_sb = sb("lin_sb", [P, PC, D])
        linb_sb = sb("linb_sb", [1, D])
        bias_cols = sb("bias_cols", [P, PC, T])
        bias_sb = sb("bias_sb", [T, D])
        affw_sb = sb("affw_sb", [T, D])
        base_sb = sb("base_sb", [T, D])
        pos_sb = sb("pos_sb", [T, D])
        wqkv_sb = sb("wqkv_sb", [P, DC, 3 * D])
        wout_sb = sb("wout_sb", [P, DC, D])
        wg_sb = sb("wg_sb", [P, DC, E])
        ones = sb("ones", [P, P])
        neg_half = sb("neg_half", [P, 1])

        scores = sb("scores", [E, NT * T])
        w1_sb = slots("w1_sb", [P, DC, HID], n=NW)
        w3_sb = slots("w3_sb", [P, DC, HID], n=NW)
        w2_sb = slots("w2_sb", [P, HC, D], n=NW)

        lasting = ctx
        ctx = lasting.enter_context(ExitStack())
        x_in = slots("x_in", [T, PD])
        x_t = slots("x_t", [P, PC, T])
        y = slots("y", [T, D])
        h = slots("h", [T, D])
        xa = slots("xa", [T, D])
        xa_t = slots("xa_t", [P, DC, T])
        qk = slots("qk", [T, 2 * D])
        v1 = slots("v1", [T, HEADS, HD + 1])
        rope_a = sb("rope_a", [T, 2 * D])
        rope_b = sb("rope_b", [T, 2 * D])
        qkr = slots("qkr", [T, 2 * D])
        expo = slots("expo", [T, 2 * D])
        feat = slots("feat", [T, 2 * D])
        k_t = slots("k_t", [P, DC, T])
        q_masked = sb("q_masked", [P, DC, HPC, T])
        s_t = slots("s_t", [T, HEADS, T])
        den = slots("den", [T, 2, HEADS])
        att = slots("att", [T, D])
        att_t = slots("att_t", [P, DC, T])
        h2 = slots("h2", [T, D])
        row = slots("row", [T, ROW])
        x2_t = slots("x2_t", [P, DC, T])
        stat = {n: slots(f"stat_{n}", [T, 12]) for n in ("ln1", "ln2", "ln3", "ln4")}
        mean_var = {n: slots(f"mv_{n}", [T, 2]) for n in ("ln1", "ln2", "ln3", "ln4")}
        var_eps = {n: slots(f"ve_{n}", [T, 1]) for n in ("ln1", "ln2", "ln3", "ln4")}
        rstd = {n: slots(f"rstd_{n}", [T, 1]) for n in ("ln1", "ln2", "ln3", "ln4")}

        ctx.close()
        ctx = lasting

        bank = [ctx.enter_context(nc.psum_tensor(f"bank{k}", [P, 512], F32)) for k in range(8)]
        S_BANKS = bank[0:3]
        B3, B4, B5, B6, B7 = bank[3:8]

        const_loaded = sem("const_loaded")
        setup = sem("setup")
        bias_summed = sem("bias_summed")
        pool_ready = sem("pool_ready")
        x_loaded = sems("x_loaded", UNROLL)
        h2_stored = sems("h2_stored", UNROLL)
        row_stored = sems("row_stored", UNROLL)
        LN_STEPS = 4
        ln = {n: sem(f"dve_{n}") for n in ("ln1", "ln2", "ln3", "ln4")}
        rs = {n: sem(f"pool_{n}") for n in ("ln1", "ln2", "ln3", "ln4")}
        biased = sem("biased")
        affined = sem("affined")
        turned = sem("turned")
        roped = sem("roped")
        rectified = sem("rectified")
        feat_ready = sem("feat_ready")
        q_ready = sem("q_ready")
        s_masked = sem("s_masked")
        att_steps = sem("att_steps")
        h2_ready = sem("h2_ready")
        sc_copied = sem("sc_copied")
        pe_xt, pe_y, pe_xat, pe_qk, pe_v, pe_qkt, pe_s, pe_av, pe_at, pe_o, pe_x2t, pe_sc, pe_sct = (
            sem(n) for n in ("pe_xt", "pe_y", "pe_xat", "pe_qk", "pe_v", "pe_qkt", "pe_s", "pe_av", "pe_at",
                             "pe_o", "pe_x2t", "pe_sc", "pe_sct"))
        a_xt, a_xat, a_qk, a_v, a_at, a_x2t, a_sct = (
            sem(n) for n in ("a_xt", "a_xat", "a_qk", "a_v", "a_at", "a_x2t", "a_sct"))
        N_CONST = 13

        w_loaded = sems("w_loaded", NW)
        sc128 = sb("sc128", [P, F])
        yv = sb("yv", [P, F])
        junk = sb("junk", [P, F])
        below = sb("below", [P, 3, F])
        sel_gt = sb("sel_gt", [P, F])
        sel_eq = sb("sel_eq", [P, F])
        scan = sb("scan", [P, F])
        picked = sb("picked", [P, F])
        ex = sb("ex", [P, F])
        zeros = sb("zeros", [P, F])
        cnt = sb("cnt", [P, 8], BF16)
        col = sb("col", [P, 16])
        t_int = sb("t_int", [P, 1], I32)
        a_int = sb("a_int", [P, 1], I32)
        cand = sb("cand", [P, 3], I32)
        junk3 = sb("junk3", [P, 3])
        block_ones = sb("block_ones", [P, P], BF16)
        block_tri = sb("block_tri", [P, P], BF16)
        diag_max = sb("diag_max", [P, P])
        max8 = sb("max8", [P, E])
        neg_max8 = sb("neg_max8", [P, E])
        e8 = sb("e8", [P, E])
        rz8 = sb("rz8", [P, E])
        slot_t = sb("slot_t", [FH, 2 * P], I32)
        hi_t = sb("hi_t", [FH, 2 * P], I32)
        lo_t = sb("lo_t", [FH, 2 * P], I32)
        hot_hi = sb("hot_hi", [FH, 2 * P, HI], BF16)
        hot_lo = sb("hot_lo", [FH, 2 * P, LO], BF16)
        hot_id = sb("hot_id", [FH, 2 * P, 2, LO], BF16)
        u_bf = sb("u_bf", [FH, 2 * P], BF16)
        id_f = sb("id_f", [HI, E, LO])
        id_u = sb("id_u", [HI, E, LO], U32)
        ids = sb("ids", [SP_, E, ST], U32)
        xg = slots("xg", [SP_, ST, ROW], n=2)
        xg_t = slots("xg_t", [P, DC, CAP], n=2)
        gate = slots("gate", [P, CAP], n=2)
        hid = slots("hid", [P, HC, CAP], n=2)
        w_slot = slots("w_slot", [SP_, ST, 2], n=2)
        y_w = slots("y_w", [SP_, ST, D], n=2)

        scores_out = sem("scores_out")
        scores_in = sem("scores_in")
        topk = sem("topk")
        pe_cnt = sem("pe_cnt")
        act_ex = sem("act_ex")
        pe_tk = sem("pe_tk")
        ids_out = sem("ids_out")
        ids_in = sem("ids_in")
        gathered = sems("gathered", 2)
        scattered = sem("scattered")
        pe_xgt = sem("pe_xgt")
        a_xgt = sem("a_xgt")
        pe_h = sem("pe_h")
        a_gate = sem("a_gate")
        hid_ready = sem("hid_ready")
        pe_y2 = sem("pe_y2")
        a_exp = sem("a_exp")
        w_ready = sem("w_ready")
        y_ready = sem("y_ready")

        def width(t):
            return LAST if isinstance(t.i, int) and t.i == NT - 1 else T

        def rows_of(dram, t, n):
            return dram[t.i * T:t.i * T + n, :] if isinstance(t.i, int) else dram[bass.ds(t.i * T, n), :]

        x_flat = x.rearrange("n t f -> (n t) f")
        out_flat = out.rearrange("b n d -> (b n) d")

        block = ctx.enter_context(nc.Block())

        @block.sync
        def _(sp):
            sp.dma_start(cf[:], consts).then_inc(const_loaded, 16)
            sp.dma_start(ci[:], consts_i).then_inc(const_loaded, 16)
            sp.dma_start(ln1_sb[:], ln1).then_inc(const_loaded, 16)
            sp.dma_start(lin_sb[:], lin_w.rearrange("(c p) d -> p c d", p=P)).then_inc(const_loaded, 16)
            sp.dma_start(linb_sb[:], lin_b).then_inc(const_loaded, 16)
            sp.dma_start(affw_sb[:], affine_w).then_inc(const_loaded, 16)
            sp.dma_start(base_sb[:], base).then_inc(const_loaded, 16)
            sp.dma_start(pos_sb[:], pos).then_inc(const_loaded, 16)
            sp.dma_start(wqkv_sb[:], w_qkv.rearrange("(c p) d -> p c d", p=P)).then_inc(const_loaded, 16)
            sp.dma_start(wout_sb[:], w_out.rearrange("(c p) d -> p c d", p=P)).then_inc(const_loaded, 16)
            sp.dma_start(wg_sb[:], wg.rearrange("(c p) e -> p c e", p=P)).then_inc(const_loaded, 16)

            def load_expert(e):
                w = e % NW
                sp.dma_start(w1_sb[w][:], w1[e].rearrange("(c p) h -> p c h", p=P)).then_inc(w_loaded[w], 16)
                sp.dma_start(w3_sb[w][:], w3[e].rearrange("(c p) h -> p c h", p=P)).then_inc(w_loaded[w], 16)
                sp.dma_start(w2_sb[w][:], w2[e].rearrange("(m p) d -> p m d", p=P)).then_inc(w_loaded[w], 16)

            def step(tiles):
                t = tiles[0]
                if t:
                    if not isinstance(t.i, int) or t.i >= UNROLL:
                        sp.wait_ge(pe_xt, t.i - (UNROLL - 1))
                    sp.dma_start(x_in[t.slot][:], rows_of(x_flat, t, T)).then_inc(x_loaded[t.slot], 16)
                t = tiles[4]
                if t:
                    n = width(t)
                    sp.wait_ge(h2_ready, t.i + 1)
                    sp.dma_start(rows_of(out_flat, t, n), h2[t.slot][0:n, :]).then_inc(h2_stored[t.slot], 16)
                    sp.wait_ge(sc_copied, t.i + 1)
                    sp.dma_start(rows_of(rows_dram, t, T), row[t.slot][:]).then_inc(row_stored[t.slot], 16)

            run_steps(sp, step)
            for e in range(NW):
                load_expert(e)
            sp.wait_ge(a_sct, NT)
            sp.dma_start(scores_dram, scores[:, 0:TOKENS]).then_inc(scores_out, 16)
            sp.wait_ge(scores_out, 16)
            sp.dma_start(sc128[:], scores_dram.rearrange("e (j f) -> (e j) f", j=J)).then_inc(scores_in, 16)
            sp.wait_ge(topk, TK_IDS)
            sp.dma_start(ids_dram.rearrange("e (hi lo) -> hi e lo", lo=LO), id_u[:]).then_inc(ids_out, 16)
            sp.wait_ge(ids_out, 16)
            sp.dma_start(ids[:], ids_dram[:, 0:SP_ * ST].rearrange("e (p s) -> p e s", s=ST)).then_inc(ids_in, 16)
            for e in range(NW, E):
                sp.wait_ge(pe_y2, ST * (e - NW + 1))
                load_expert(e)

        @block.tensor
        def _(pe):
            pe.wait_ge(setup, 2)
            for c in range(PC):
                pe.matmul(B7[0:T, 0:D], bias_cols[:, c, :], lin_sb[:, c, :], start=(c == 0), stop=False)
            pe.matmul(B7[0:T, 0:D], ones[0:1, 0:T], linb_sb[:], start=False, stop=True).then_inc(bias_summed, 1)

            def turn(o, src, chunks, rows=T):
                for c in range(chunks):
                    mm = pe.transpose(o(c), src[:, c * P:(c + 1) * P], ident[0:rows, 0:rows])
                return mm

            def weigh_values(t, heads):
                for n in heads:
                    mm = pe.matmul(B6[0:T, n * (HD + 1):(n + 1) * (HD + 1)], s_t[t.slot][:, n, :],
                                   v1[t.slot][:, n, :], start=True, stop=True)
                return mm

            def values_ready(t, former):
                pe.wait_ge(s_masked, 4 * t.i + 4)
                pe.wait_ge(a_v, t.i + 1)
                if former:
                    pe.wait_ge(sc_copied, t.i)

            def score(t, b):
                g, c = b // 2, b % 2
                pe.wait_ge(q_ready, 2 * t.i + g + 1)
                if b >= len(S_BANKS):
                    pe.wait_ge(s_masked, 4 * t.i + b - len(S_BANKS) + 1)
                pe.matmul(S_BANKS[b % len(S_BANKS)][0:T, 0:HB * T], k_t[t.slot][:, c, :],
                          q_masked[:, c, g * HB:(g + 1) * HB, :], start=True, stop=True).then_inc(pe_s, 1)

            def step(tiles):
                t0, t1, t2, t3, t4 = tiles
                if t1:
                    pe.wait_ge(a_xt, t1.i + 1)
                    if isinstance(t1.i, int) and t1.i == 0:
                        pe.wait_ge(setup, 4)
                    else:
                        pe.wait_ge(a_qk, t1.i)
                    for c in range(PC):
                        mm = pe.matmul(B7[0:T, 0:D], x_t[t1.slot][:, c, :], lin_sb[:, c, :],
                                       start=(c == 0), stop=(c == PC - 1))
                        if t3 and c == 0:
                            values_ready(t3, t4)
                        if t3 and c < PC - 1:
                            weigh_values(t3, EARLY_HEADS[c])
                    mm.then_inc(pe_y, 1)
                elif t3:
                    values_ready(t3, t4)
                    weigh_values(t3, range(0, AV_EARLY))
                if t2:
                    pe.wait_ge(feat_ready, t2.i + 1)
                    turn(lambda c: B5[:, c * T:(c + 1) * T], feat[t2.slot], 2 * DC).then_inc(pe_qkt, 1)
                if t3:
                    weigh_values(t3, range(AV_EARLY, HEADS)).then_inc(pe_av, 1)
                if t2:
                    score(t2, 0)
                    score(t2, 1)
                if t3:
                    pe.wait_ge(att_steps, 3 * t3.i + 3)
                    turn(lambda c: B4[:, c * T:(c + 1) * T], att[t3.slot], DC).then_inc(pe_at, 1)
                if t4:
                    pe.wait_ge(sc_copied, t4.i + 1)
                    pe.transpose(B4[0:E, DC * T:(DC + 1) * T], row[t4.slot][:, D:ROW],
                                 ident[0:T, 0:T]).then_inc(pe_sct, 1)
                if t2:
                    score(t2, 2)
                if t3:
                    pe.wait_ge(a_at, t3.i + 1)
                    for c in range(DC):
                        mm = pe.matmul(B6[0:T, 0:D], att_t[t3.slot][:, c, :], wout_sb[:, c, :],
                                       start=(c == 0), stop=(c == DC - 1))
                    mm.then_inc(pe_o, 1)
                if t1:
                    pe.wait_ge(ln["ln3"], LN_STEPS * t1.i + 4)
                    if t2:
                        pe.wait_ge(q_ready, 2 * t2.i + 2)
                    turn(lambda c: B5[:, c * T:(c + 1) * T], xa[t1.slot], DC).then_inc(pe_xat, 1)
                if t2:
                    score(t2, 3)
                if t1:
                    pe.wait_ge(a_xat, t1.i + 1)
                    for c in range(DC):
                        mm = pe.matmul(B7[0:T, 0:2 * D], xa_t[t1.slot][:, c, :], wqkv_sb[:, c, 0:2 * D],
                                       start=(c == 0), stop=(c == DC - 1))
                    mm.then_inc(pe_qk, 1)
                if t0:
                    pe.wait_ge(ln["ln1"], LN_STEPS * t0.i + 4)
                    if t4:
                        pe.wait_ge(a_sct, t4.i + 1)
                    turn(lambda c: B4[:, c * T:(c + 1) * T] if c < 4 else B5[:, (c - 4) * T:(c - 3) * T],
                         x_in[t0.slot], PC).then_inc(pe_xt, 1)
                if t3:
                    pe.wait_ge(ln["ln4"], LN_STEPS * t3.i + 4)
                    turn(lambda c: B6[:, D + c * T:D + (c + 1) * T], row[t3.slot], DC).then_inc(pe_x2t, 1)
                if t1:
                    for c in range(DC):
                        mm = pe.matmul(B3[0:T, 0:D], xa_t[t1.slot][:, c, :], wqkv_sb[:, c, 2 * D:3 * D],
                                       start=(c == 0), stop=(c == DC - 1))
                    mm.then_inc(pe_v, 1)
                if t3:
                    pe.wait_ge(a_x2t, t3.i + 1)
                    for c in range(DC):
                        mm = pe.matmul(B6[0:T, 0:E], x2_t[t3.slot][:, c, :], wg_sb[:, c, :],
                                       start=(c == 0), stop=(c == DC - 1))
                    mm.then_inc(pe_sc, 1)

            run_steps(pe, step)

            def count(n, lhs, rhs, o, dve_at):
                pe.wait_ge(topk, dve_at)
                pe.matmul(o, lhs, rhs, start=True, stop=True).then_inc(pe_cnt, 1)

            pe.wait_ge(sc_copied, NT)
            pe.wait_ge(a_sct, NT)
            count(0, block_ones[:], cnt[:, 0:1], B7[:, 0:1], TK_SIGN)
            count(1, ones[:], diag_max[:], B6[:, 0:P], TK_MAX)
            with pe.Fori(0, SEARCH) as r:
                pe.wait_ge(topk, TK_SEARCH + TK_ROUND * r + 2)
                pe.matmul(B7[:, 0:3], block_ones[:], cnt[:, 1:4], start=True, stop=True).then_inc(pe_cnt, 1)
            count(0, block_ones[:], cnt[:, 1:2], B7[:, 0:1], TK_LAST + 2)
            pe.wait_ge(topk, TK_GT)
            pe.matmul(B7[:, 0:1], block_ones[:], cnt[:, 4:5], start=True, stop=True)
            pe.matmul(B7[:, 1:2], block_tri[:], cnt[:, 5:6], start=True, stop=True).then_inc(pe_cnt, 1)
            count(0, block_tri[:], cnt[:, 6:7], B7[:, 0:1], TK_SEL)
            pe.wait_ge(topk, TK_Z)
            pe.matmul(B6[:, 0:E], ones[:], e8[:], start=True, stop=True).then_inc(pe_cnt, 1)
            pe.wait_ge(topk, TK_POS)
            for c in range(2):
                mm = pe.transpose(B4[0:FH, c * P:(c + 1) * P], picked[:, c * FH:(c + 1) * FH], ident)
            mm.then_inc(pe_cnt, 1)
            pe.wait_ge(topk, TK_HOT)
            for e in range(E):
                for n in range(2 * J):
                    k = (n // J) * P + e * J + n % J
                    mm = pe.matmul(B5[0:HI, e * 2 * LO:(e + 1) * 2 * LO], hot_hi[:, k, :],
                                   hot_id[:, k, :, :], start=(n == 0), stop=(n == 2 * J - 1))
            mm.then_inc(pe_cnt, 1)

            def up(e):
                pe.wait_ge(gathered[e % 2], 16 * ST * (e // 2 + 1))
                if e >= 1:
                    pe.wait_ge(a_xgt, 2 * e)
                for c in range(DC):
                    for s in range(ST):
                        n = min(SP_, CAP - s * SP_)
                        mm = pe.transpose(bank[c][:, s * SP_:s * SP_ + n], xg[e % 2][0:n, s, c * P:(c + 1) * P],
                                          ident[0:n, 0:n])
                    mm.then_inc(pe_xgt, 1)

            def hidden(e):
                pe.wait_ge(w_loaded[e % NW], 48 * (e // NW + 1))
                pe.wait_ge(a_xgt, 2 * (e + 1))
                for m in range(HC):
                    k = HC * e + m
                    if k >= 2:
                        pe.wait_ge(hid_ready, k - 1)
                    g, u = bank[2 + 2 * (k % 2)], bank[3 + 2 * (k % 2)]
                    for c in range(DC):
                        pe.matmul(g[:, 0:CAP], w1_sb[e % NW][:, c, m * P:(m + 1) * P], xg_t[e % 2][:, c, :],
                                  start=(c == 0), stop=(c == DC - 1))
                    for c in range(DC):
                        mm = pe.matmul(u[:, 0:CAP], w3_sb[e % NW][:, c, m * P:(m + 1) * P], xg_t[e % 2][:, c, :],
                                       start=(c == 0), stop=(c == DC - 1))
                    mm.then_inc(pe_h, 1)

            def down(e):
                pe.wait_ge(hid_ready, HC * (e + 1))
                for s in range(ST):
                    n = min(SP_, CAP - s * SP_)
                    k = ST * e + s
                    if k >= 2:
                        pe.wait_ge(y_ready, k - 1)
                    for m in range(HC):
                        mm = pe.matmul(bank[6 + k % 2][0:n, 0:D], hid[e % 2][:, m, s * SP_:s * SP_ + n],
                                       w2_sb[e % NW][:, m, :], start=(m == 0), stop=(m == HC - 1))
                    mm.then_inc(pe_y2, 1)

            pe.wait_ge(topk, TK_IDS)
            up(0)
            for e in range(E):
                hidden(e)
                if e + 1 < E:
                    up(e + 1)
                down(e)

        @block.scalar
        def _(act):
            def queries(t, n):
                return nc.scalar.activation(q_masked[:, :, n, :],
                                            B5[:, 0:DC * T].rearrange("p (c t) -> p c t", c=DC), ACT.Copy,
                                            scale=head_of[:, n:n + 1])

            def step(tiles):
                t0, t1, t2, t3, t4 = tiles
                if t2:
                    act.wait_ge(roped, ROPE * t2.i + ROPE)
                    nc.scalar.activation(expo[t2.slot][:], qkr[t2.slot][:], ACT.Exp)
                    nc.scalar.activation(qkr[t2.slot][:], qkr[t2.slot][:], ACT.Relu).then_inc(rectified, 1)
                    act.wait_ge(pe_qkt, t2.i + 1)
                    nc.scalar.copy(k_t[t2.slot][:], B5[:, DC * T:2 * DC * T])
                    for g in range(2):
                        for n in range(g * HB, (g + 1) * HB):
                            last = queries(t2, n)
                        last.then_inc(q_ready, 1)
                if t3:
                    act.wait_ge(pe_at, t3.i + 1)
                    if t4:
                        act.wait_ge(pe_sct, t4.i + 1)
                    nc.scalar.copy(att_t[t3.slot][:], B4[:, 0:DC * T]).then_inc(a_at, 1)
                if t4:
                    act.wait_ge(pe_sct, t4.i + 1)
                    o = (scores[:, t4.i * T:(t4.i + 1) * T] if isinstance(t4.i, int)
                         else scores[:, bass.ds(t4.i * T, T)])
                    nc.scalar.copy(o, B4[0:E, DC * T:(DC + 1) * T]).then_inc(a_sct, 1)
                if t1:
                    act.wait_ge(pe_xat, t1.i + 1)
                    nc.scalar.copy(xa_t[t1.slot][:], B5[:, 0:DC * T]).then_inc(a_xat, 1)
                    act.wait_ge(pe_qk, t1.i + 1)
                    nc.scalar.copy(qk[t1.slot][:], B7[0:T, 0:2 * D]).then_inc(a_qk, 1)
                if t0:
                    act.wait_ge(pe_xt, t0.i + 1)
                    nc.scalar.copy(x_t[t0.slot][:, 0:4, :], B4[:, 0:4 * T])
                    nc.scalar.copy(x_t[t0.slot][:, 4:PC, :], B5[:, 0:(PC - 4) * T]).then_inc(a_xt, 1)
                if t3:
                    act.wait_ge(pe_x2t, t3.i + 1)
                    nc.scalar.copy(x2_t[t3.slot][:], B6[:, D:D + DC * T]).then_inc(a_x2t, 1)
                if t1:
                    act.wait_ge(pe_v, t1.i + 1)
                    nc.scalar.copy(v1[t1.slot][:, :, 0:HD],
                                   B3[0:T, 0:D].rearrange("t (n d) -> t n d", n=HEADS)).then_inc(a_v, 1)

            act.wait_ge(setup, 4)
            run_steps(act, step)

            act.wait_ge(topk, TK_MAXOWN)
            nc.scalar.activation(ex[:], sc128[:], ACT.Exp, bias=col[:, 5:6]).then_inc(act_ex, 1)

            for e in range(E):
                act.wait_ge(gathered[e % 2], 16 * ST * (e // 2 + 1))
                if e == 0:
                    act.wait_ge(topk, TK_IDS)
                if e >= 2:
                    act.wait_ge(y_ready, ST * (e - 1))
                for s in range(ST):
                    n = min(SP_, CAP - s * SP_)
                    last = nc.scalar.activation(w_slot[e % 2][0:n, s, 0:1], xg[e % 2][0:n, s, D + e:D + e + 1],
                                                ACT.Exp, bias=neg_max8[0:n, e:e + 1])
                last.then_inc(a_exp, 1)
                for c in range(DC):
                    act.wait_ge(pe_xgt, 2 * e + c + 1)
                    nc.scalar.copy(xg_t[e % 2][:, c, :], bank[c][:, 0:CAP]).then_inc(a_xgt, 1)
                for m in range(HC):
                    k = HC * e + m
                    act.wait_ge(pe_h, k + 1)
                    if k >= 2:
                        act.wait_ge(hid_ready, k - 1)
                    nc.scalar.activation(gate[k % 2][:], bank[2 + 2 * (k % 2)][:, 0:CAP], ACT.Silu).then_inc(a_gate, 1)

        @block.vector
        def _(dve):
            V = nc.vector
            n_setup = [0]

            def setup_step(ins):
                n_setup[0] += 1
                ins.then_inc(setup, 1)

            V.memset(ones[:], 1.0)
            for k in range(UNROLL):
                V.memset(v1[k][:], 1.0)
            setup_step(V.memset(neg_half[:], -0.5))
            dve.wait_ge(setup, 1)
            dve.wait_ge(const_loaded, 16 * 11)
            for c in range(PC):
                last = V.tensor_scalar(bias_cols[:, c, :], ones[:, 0:T], ln1_sb[:, 1, c:c + 1], None, ALU.mult)
            setup_step(last)
            V.tensor_tensor(base_sb[:], base_sb[:], pos_sb[:], ALU.add)
            dve.wait_ge(bias_summed, 1)
            V.tensor_copy(bias_sb[:], B7[0:T, 0:D]).then_inc(setup, 1)
            for c in range(PC):
                last = V.tensor_scalar(lin_sb[:, c, :], lin_sb[:, c, :], ln1_sb[:, 0, c:c + 1], None, ALU.mult)
            last.then_inc(setup, 1)
            dve.wait_ge(setup, 4)

            def ln_stats(n, t, src, width):
                parts = -(-width // 512)
                w = width // parts
                for k in range(parts):
                    last = V.bn_stats(stat[n][t.slot][:, 6 * k:6 * k + 6], src[:, k * w:(k + 1) * w])
                last.then_inc(ln[n], 1)
                dve.wait_ge(ln[n], LN_STEPS * t.i + 1)
                V.memset(var_eps[n][t.slot][:], EPS)
                V.bn_aggr(mean_var[n][t.slot][:], stat[n][t.slot][:, 0:6 * parts]).then_inc(ln[n], 1)
                dve.wait_ge(ln[n], LN_STEPS * t.i + 2)
                V.tensor_tensor(var_eps[n][t.slot][:], var_eps[n][t.slot][:], mean_var[n][t.slot][:, 1:2],
                                ALU.add).then_inc(ln[n], 1)

            def ln_scale(n, t, dst, src):
                dve.wait_ge(rs[n], t.i + 1)
                V.tensor_scalar(dst, src, mean_var[n][t.slot][:, 0:1], rstd[n][t.slot][:], ALU.subtract,
                                ALU.mult).then_inc(ln[n], 1)

            def mask_scores(t, b):
                g, c = b // 2, b % 2
                n = c * HPC + g * HB
                dve.wait_ge(pe_s, 4 * t.i + b + 1)
                V.tensor_tensor(s_t[t.slot][:, n:n + HB, :],
                                S_BANKS[b % len(S_BANKS)][0:T, 0:HB * T].rearrange("s (n t) -> s n t", n=HB),
                                causal.unsqueeze(1).broadcast_to([T, HB, T]), ALU.mult).then_inc(s_masked, 1)

            def step(tiles):
                t0, t1, t2, t3, t4 = tiles
                if t0:
                    dve.wait_ge(x_loaded[t0.slot], 16 * t0.q + 16)
                    ln_stats("ln1", t0, x_in[t0.slot], PD)
                if t2:
                    dve.wait_ge(rectified, t2.i + 1)
                    V.scalar_tensor_tensor(out=feat[t2.slot][:], in0=expo[t2.slot][:], scalar=1.0,
                                           in1=qkr[t2.slot][:], op0=ALU.min, op1=ALU.add).then_inc(feat_ready, 1)
                if t1:
                    dve.wait_ge(pe_y, t1.i + 1)
                    V.tensor_tensor(y[t1.slot][:], B7[0:T, 0:D], bias_sb[:], ALU.add).then_inc(biased, 1)
                    dve.wait_ge(biased, t1.i + 1)
                    ln_stats("ln2", t1, y[t1.slot], D)
                    V.scalar_tensor_tensor(out=y[t1.slot][:], in0=y[t1.slot][:],
                                           scalar=mean_var["ln2"][t1.slot][:, 0:1], in1=affw_sb[:],
                                           op0=ALU.subtract, op1=ALU.mult).then_inc(ln["ln2"], 1)
                if t3:
                    dve.wait_ge(pe_av, t3.i + 1)
                    o = B6[0:T, 0:HEADS * (HD + 1)].rearrange("t (n d) -> t n d", n=HEADS)
                    V.tensor_scalar(den[t3.slot][:, 0, :], o[:, :, HD], 1e-6, None, ALU.max).then_inc(att_steps, 1)
                    dve.wait_ge(att_steps, 3 * t3.i + 1)
                    V.reciprocal(den[t3.slot][:, 1, :], den[t3.slot][:, 0, :]).then_inc(att_steps, 1)
                    dve.wait_ge(att_steps, 3 * t3.i + 2)
                    V.tensor_tensor(att[t3.slot][:].rearrange("t (n d) -> t n d", n=HEADS), o[:, :, 0:HD],
                                    den[t3.slot][:, 1, :].unsqueeze(2).broadcast_to([T, HEADS, HD]),
                                    ALU.mult).then_inc(att_steps, 1)
                if t1:
                    dve.wait_ge(rs["ln2"], t1.i + 1)
                    dve.wait_ge(ln["ln2"], LN_STEPS * t1.i + 4)
                    V.scalar_tensor_tensor(out=h[t1.slot][:], in0=y[t1.slot][:], scalar=rstd["ln2"][t1.slot][:],
                                           in1=base_sb[:], op0=ALU.mult, op1=ALU.add).then_inc(affined, 1)
                    dve.wait_ge(affined, t1.i + 1)
                    ln_stats("ln3", t1, h[t1.slot], D)
                if t0:
                    ln_scale("ln1", t0, x_in[t0.slot][:], x_in[t0.slot][:])
                if t1:
                    ln_scale("ln3", t1, xa[t1.slot][:], h[t1.slot][:])
                if t2:
                    mask_scores(t2, 0)
                    mask_scores(t2, 1)
                    mask_scores(t2, 2)
                if t3:
                    dve.wait_ge(pe_o, t3.i + 1)
                    if not isinstance(t3.i, int) or t3.i >= UNROLL:
                        dve.wait_ge(h2_stored[t3.slot], 16 * t3.q)
                        dve.wait_ge(row_stored[t3.slot], 16 * t3.q)
                    V.tensor_tensor(h2[t3.slot][:], B6[0:T, 0:D], h[t3.slot][:], ALU.add).then_inc(h2_ready, 1)
                    dve.wait_ge(h2_ready, t3.i + 1)
                    ln_stats("ln4", t3, h2[t3.slot], D)
                if t2:
                    mask_scores(t2, 3)
                if t3:
                    ln_scale("ln4", t3, row[t3.slot][:, 0:D], h2[t3.slot][:])
                if t1:
                    dve.wait_ge(a_qk, t1.i + 1)
                    if not isinstance(t1.i, int) or t1.i >= 1:
                        dve.wait_ge(roped, ROPE * t1.i)
                    V.tensor_tensor(rope_a[:], qk[t1.slot][:], cos_t, ALU.mult).then_inc(turned, 1)
                if t3:
                    dve.wait_ge(pe_sc, t3.i + 1)
                    V.tensor_copy(row[t3.slot][:, D:ROW], B6[0:T, 0:E]).then_inc(sc_copied, 1)

            run_steps(dve, step)

            at = [0]

            def link(ins):
                at[0] += 1
                ins.then_inc(topk, 1)
                dve.wait_ge(topk, at[0])

            def mark(name):
                assert at[0] == name, (at[0], name)

            sgn, lim, t_s, need, nmax_own, acc, zc, soff, eoff, g_tot = (col[:, k:k + 1] for k in (0, 1, 2, 3, 5, 6, 7, 8, 9, 10))
            for k in range(UNROLL):
                n = len(range(k, NT, UNROLL))
                dve.wait_ge(h2_stored[k], 16 * n)
                dve.wait_ge(row_stored[k], 16 * n)
            V.memset(zeros[:], 0.0)
            V.memset(t_int[:], 0)
            V.tensor_copy(block_ones[:], ci[:, I_BLOCK:I_BLOCK + P])
            V.tensor_copy(block_tri[:], ci[:, I_TRI:I_TRI + P])
            V.tensor_copy(u_bf[:], ci[0:FH, I_U:I_U + 2 * P])
            dve.wait_ge(scores_in, 16)
            link(V.tensor_scalar(junk[:], sc128[:], 0.0, None, ALU.is_ge, ALU.add, accum_out=cnt[:, 0:1]))
            mark(TK_SIGN)
            link(V.reduce_max(acc, sc128[:], AX.X))
            link(V.tensor_scalar(diag_max[:], ident, acc, None, ALU.mult))
            mark(TK_MAX)
            dve.wait_ge(pe_cnt, 1)
            link(V.tensor_scalar(lim, B7[:, 0:1], float(CAP), 2.0, ALU.is_ge, ALU.mult))
            link(V.tensor_scalar(sgn, lim, -1.0, None, ALU.add))
            link(V.tensor_scalar(lim, sgn, (TOKENS - 2 * CAP + 1) / 2, (TOKENS - 1) / 2, ALU.mult, ALU.add))
            link(V.tensor_scalar(yv[:], sc128[:], sgn, None, ALU.mult))
            dve.wait_ge(pe_cnt, 2)
            link(V.reduce_max(max8[:], B6[:, 0:P].rearrange("p (e j) -> p e j", e=E), AX.X))
            link(V.tensor_scalar(neg_max8[:], max8[:], -1.0, None, ALU.mult))
            link(V.tensor_tensor(e8[:], neg_max8[:], expert_of, ALU.mult))
            link(V.reduce_sum(nmax_own, e8[:], AX.X))
            mark(TK_MAXOWN)
            mark(TK_SEARCH)

            def search(tab, scale, n, k, pe_k):
                V.tensor_tensor(cand[:, 0:n], t_int[:].broadcast_to([P, n]), tab, ALU.bitwise_or).then_inc(topk, 1)
                dve.wait_ge(topk, k + 1)
                for c in range(n):
                    last = V.tensor_scalar(below[:, c, :], yv[:], cand[:, c:c + 1].bitcast(F32), None, ALU.is_lt,
                                           ALU.add, accum_out=cnt[:, 1 + c:2 + c])
                last.then_inc(topk, 1)
                dve.wait_ge(pe_cnt, pe_k)
                V.tensor_scalar(junk3[:, 0:n], B7[:, 0:n], lim, None, ALU.is_le, ALU.add,
                                accum_out=acc).then_inc(topk, 1)
                dve.wait_ge(topk, k + 3)
                V.tensor_scalar(a_int[:], acc, scale, None, ALU.mult).then_inc(topk, 1)
                dve.wait_ge(topk, k + 4)
                V.tensor_tensor(t_int[:], t_int[:], a_int[:], ALU.bitwise_or).then_inc(topk, 1)
                dve.wait_ge(topk, k + 5)

            with dve.Fori(0, SEARCH) as r:
                search(ci[:, bass.ds(3 * r + I_BITS, 3)], cf[:, bass.ds(r + C_SCALE, 1)], 3,
                       TK_ROUND * r + TK_SEARCH, r + 3)
            search(ci[:, I_LO + 1:I_LO + 2], 1.0, 1, TK_LAST, 3 + SEARCH)
            at[0] = TK_LAST + TK_ROUND
            n_pe = 3 + SEARCH
            link(V.tensor_scalar(t_s, t_int[:].bitcast(F32), sgn, None, ALU.mult))
            V.tensor_scalar(sel_gt[:], sc128[:], t_s, None, ALU.is_gt, ALU.add, accum_out=cnt[:, 4:5])
            link(V.tensor_scalar(sel_eq[:], sc128[:], t_s, None, ALU.is_equal, ALU.add, accum_out=cnt[:, 5:6]))
            mark(TK_GT)
            dve.wait_ge(pe_cnt, n_pe + 1)
            V.tensor_copy(eoff, B7[:, 1:2])
            link(V.tensor_scalar(need, B7[:, 0:1], -1.0, float(CAP), ALU.mult, ALU.add))
            link(V.tensor_tensor_scan(scan[:], sel_eq[:], zeros[:], eoff, ALU.add, ALU.add))
            link(V.scalar_tensor_tensor(out=junk[:], in0=scan[:], scalar=need, in1=sel_eq[:], op0=ALU.is_le,
                                        op1=ALU.mult))
            link(V.scalar_tensor_tensor(out=picked[:], in0=junk[:], scalar=0.0, in1=sel_gt[:], op0=ALU.add,
                                        op1=ALU.add, accum_out=cnt[:, 6:7]))
            mark(TK_SEL)
            dve.wait_ge(act_ex, 1)
            link(V.scalar_tensor_tensor(out=junk[:], in0=ex[:], scalar=1.0, in1=picked[:], op0=ALU.mult,
                                        op1=ALU.mult, accum_out=zc))
            link(V.tensor_scalar(e8[:], expert_of, zc, None, ALU.mult))
            mark(TK_Z)
            dve.wait_ge(pe_cnt, n_pe + 2)
            link(V.tensor_copy(soff, B7[:, 0:1]))
            link(V.tensor_tensor_scan(scan[:], picked[:], zeros[:], soff, ALU.add, ALU.add))
            link(V.tensor_tensor(picked[:], picked[:], scan[:], ALU.mult))
            mark(TK_POS)
            dve.wait_ge(pe_cnt, n_pe + 3)
            link(V.reciprocal(rz8[:], B6[:, 0:E]))
            dve.wait_ge(pe_cnt, n_pe + 4)
            link(V.tensor_scalar(slot_t[:], B4[0:FH, 0:2 * P], -1.0, None, ALU.add))
            link(V.tensor_scalar(hi_t[:], slot_t[:], 4, None, ALU.arith_shift_right))
            link(V.tensor_scalar(lo_t[:], slot_t[:], LO - 1, None, ALU.bitwise_and))
            V.tensor_tensor(hot_hi[:], hi_t[:].unsqueeze(2).broadcast_to([FH, 2 * P, HI]),
                            ci[0:FH, I_HI:I_HI + HI].unsqueeze(1).broadcast_to([FH, 2 * P, HI]), ALU.is_equal)
            link(V.tensor_tensor(hot_lo[:], lo_t[:].unsqueeze(2).broadcast_to([FH, 2 * P, LO]),
                                 ci[0:FH, I_LO:I_LO + LO].unsqueeze(1).broadcast_to([FH, 2 * P, LO]), ALU.is_equal))
            V.tensor_scalar(hot_id[:, :, 0, :], hot_lo[:], cf[0:FH, C_FROW:C_FROW + 1], None, ALU.mult)
            link(V.tensor_tensor(hot_id[:, :, 1, :], hot_lo[:],
                                 u_bf[:].unsqueeze(2).broadcast_to([FH, 2 * P, LO]), ALU.mult))
            mark(TK_HOT)
            dve.wait_ge(pe_cnt, n_pe + 5)
            o = B5[0:HI, 0:E * 2 * LO].rearrange("h (e k l) -> h e k l", e=E, k=2)
            link(V.tensor_copy(id_f[:], o[:, :, 0, :]))
            link(V.scalar_tensor_tensor(out=id_u[:], in0=o[:, :, 1, :], scalar=float(FH), in1=id_f[:],
                                        op0=ALU.mult, op1=ALU.add))
            mark(TK_IDS)

            for e in range(E):
                for m in range(HC):
                    k = HC * e + m
                    dve.wait_ge(a_gate, k + 1)
                    if m == 0 and e >= 2:
                        dve.wait_ge(pe_y2, ST * (e - 1))
                    V.tensor_tensor(hid[e % 2][:, m, :], gate[k % 2][:], bank[3 + 2 * (k % 2)][:, 0:CAP],
                                    ALU.mult).then_inc(hid_ready, 1)
                dve.wait_ge(a_exp, e + 1)
                if e >= 2:
                    dve.wait_ge(scattered, 16 * ST * (e - 1))
                V.tensor_scalar(w_slot[e % 2][:, 0:2, 1], w_slot[e % 2][:, 0:2, 0], rz8[0:SP_, e:e + 1], None, ALU.mult)
                n = CAP - 2 * SP_
                V.tensor_scalar(w_slot[e % 2][0:n, 2:3, 1], w_slot[e % 2][0:n, 2:3, 0], rz8[0:n, e:e + 1], None,
                                ALU.mult).then_inc(w_ready, 1)
                dve.wait_ge(w_ready, e + 1)
                for s in range(ST):
                    n = min(SP_, CAP - s * SP_)
                    k = ST * e + s
                    dve.wait_ge(pe_y2, k + 1)
                    V.tensor_scalar(y_w[e % 2][0:n, s, :], bank[6 + k % 2][0:n, 0:D], w_slot[e % 2][0:n, s, 1:2],
                                    None, ALU.mult).then_inc(y_ready, 1)

        @block.gpsimd
        def _(pool):
            G = nc.gpsimd

            def power(n, t):
                pool.wait_ge(ln[n], LN_STEPS * t.i + 3)
                G.tensor_tensor(rstd[n][t.slot][:], var_eps[n][t.slot][:], neg_half[0:T, :], ALU.pow).then_inc(rs[n], 1)

            def halves(a):
                return a.rearrange("t (n two d) -> t n two d", two=2, d=HD // 2)

            def step(tiles):
                t0, t1, t2, t3, t4 = tiles
                if t2:
                    pool.wait_ge(a_qk, t2.i + 1)
                    if not isinstance(t2.i, int) or t2.i >= 1:
                        pool.wait_ge(roped, ROPE * t2.i)
                    a, b, s = halves(qk[t2.slot][:]), halves(rope_b[:]), halves(sin_t)
                    G.tensor_tensor(b[:, :, 0, :], a[:, :, 1, :], s[:, :, 0, :], ALU.mult).then_inc(roped, 1)
                    G.tensor_tensor(b[:, :, 1, :], a[:, :, 0, :], s[:, :, 1, :], ALU.mult).then_inc(roped, 1)
                    pool.wait_ge(turned, t2.i + 1)
                    pool.wait_ge(roped, ROPE * t2.i + 2)
                    G.tensor_tensor(qkr[t2.slot][:], rope_a[:], rope_b[:], ALU.add).then_inc(roped, 1)
                if t0:
                    power("ln1", t0)
                if t1:
                    power("ln2", t1)
                    power("ln3", t1)
                if t3:
                    power("ln4", t3)

            pool.wait_ge(setup, 4)
            run_steps(pool, step)

            def gather(e):
                if e >= 2:
                    pool.wait_ge(pe_xgt, 2 * (e - 1))
                    pool.wait_ge(a_exp, e - 1)
                for s in range(ST):
                    n = min(SP_, CAP - s * SP_)
                    G.indirect_dma_start(xg[e % 2][0:n, s, :], None, rows_dram,
                                         bass.IndirectOffsetOnAxis(ids[0:n, e, s:s + 1], 0)
                                         ).then_inc(gathered[e % 2], 16)

            def scatter(e):
                for s in range(ST):
                    n = min(SP_, CAP - s * SP_)
                    pool.wait_ge(y_ready, ST * e + s + 1)
                    if e >= 1 and s == 0:
                        pool.wait_ge(scattered, 16 * ST * e)
                    G.indirect_dma_start(out_flat, bass.IndirectOffsetOnAxis(ids[0:n, e, s:s + 1], 0),
                                         y_w[e % 2][0:n, s, :], None, compute_op=ALU.add).then_inc(scattered, 16)

            for k in range(UNROLL):
                n = len(range(k, NT, UNROLL))
                pool.wait_ge(h2_stored[k], 16 * n)
                pool.wait_ge(row_stored[k], 16 * n)
            pool.wait_ge(ids_in, 16)
            gather(0)
            gather(1)
            for e in range(E):
                scatter(e)
                if e + 2 < E:
                    gather(e + 2)
            pool.wait_ge(scattered, 16 * ST * E)


TK_SIGN = 1
TK_MAX = 3
TK_MAXOWN = 11
TK_SEARCH = 11
TK_ROUND = 5
TK_LAST = TK_SEARCH + TK_ROUND * SEARCH
TK_GT = TK_LAST + TK_ROUND + 2
TK_SEL = TK_GT + 4
TK_Z = TK_SEL + 2
TK_POS = TK_Z + 3
TK_HOT = TK_POS + 6
TK_IDS = TK_HOT + 2


def constants():
    import numpy as np

    f = np.zeros((P, NC_F), np.float32)
    i = np.zeros((P, NC_I), np.int32)
    f[:, C_ID:C_ID + P] = np.eye(P)
    r = np.arange(T)
    f[:T, C_MASK:C_MASK + T] = (r[:, None] // SEQ == r[None, :] // SEQ) & (r[:, None] <= r[None, :])
    half = HD // 2
    inv = (1.0 / np.float32(10000.0) ** (np.arange(half, dtype=np.float32) / np.float32(half))).astype(np.float32)
    ang = ((r % SEQ).astype(np.float32)[:, None] * inv[None, :]).astype(np.float32)
    scale = np.float32(HD ** -0.25)
    cos, sin = np.cos(ang) * scale, np.sin(ang) * scale
    f[:T, C_COS:C_COS + 2 * D] = np.tile(np.concatenate([cos, cos], 1), (1, 2 * HEADS))
    f[:T, C_SIN:C_SIN + 2 * D] = np.tile(np.concatenate([-sin, sin], 1), (1, 2 * HEADS))
    p = np.arange(P)
    f[:, C_HEAD:C_HEAD + HPC] = p[:, None] // HD == np.arange(HPC)[None, :]
    f[:, C_E8:C_E8 + E] = p[:, None] // J == np.arange(E)[None, :]
    for n in range(SEARCH):
        shift = 2 * (SEARCH - n) - 1
        f[:, C_SCALE + n] = 2.0 ** shift
        i[:, I_BITS + 3 * n:I_BITS + 3 * n + 3] = np.array([1, 2, 3]) << shift
    f[:, C_FROW] = p
    i[:, I_HI:I_HI + HI] = np.arange(HI)
    i[:, I_LO:I_LO + LO] = np.arange(LO)
    k = np.arange(2 * P)
    i[:, I_U:I_U + 2 * P] = 2 * (k % J) + k // P
    same = p[:, None] // J == p[None, :] // J
    i[:, I_BLOCK:I_BLOCK + P] = same
    i[:, I_TRI:I_TRI + P] = same & (p[:, None] < p[None, :])
    return f, i


def kernel(**inputs):
    import numpy as np
    import concourse.bacc as bacc
    from concourse.bass_utils import run_bass_kernel_spmd

    x = np.asarray(inputs["x"])
    n_img, chans, height, wide = x.shape
    side = 16
    rows = np.zeros((NT * IMGS, SEQ, PD), x.dtype)
    rows[:n_img, 1:] = x.reshape(n_img, chans, height // side, side, wide // side, side).transpose(
        0, 2, 4, 3, 5, 1).reshape(n_img, SEQ - 1, PD)
    ln2_w, ln2_b = np.asarray(inputs["L0_tok_ln2_w"]), np.asarray(inputs["L0_tok_ln2_b"])
    affine_w = np.zeros((IMGS, SEQ, D), ln2_w.dtype)
    affine_w[:, 1:] = ln2_w
    base = np.zeros((IMGS, SEQ, D), ln2_b.dtype)
    base[:, 1:] = ln2_b
    base[:, 0] = np.asarray(inputs["L0_tok_cls_token"])[0, 0]
    pos = np.tile(np.asarray(inputs["L0_tok_pos_embedding"])[0, :SEQ], (IMGS, 1))
    cf, ci = constants()
    data = {
        "x": rows.reshape(NT, T, PD),
        "consts": cf,
        "consts_i": ci,
        "ln1": np.stack([np.asarray(inputs["L0_tok_ln1_w"]), np.asarray(inputs["L0_tok_ln1_b"])]
                        ).reshape(2, PC, P).transpose(2, 0, 1),
        "lin_w": np.asarray(inputs["L0_tok_lin_w"]),
        "lin_b": np.asarray(inputs["L0_tok_lin_b"]).reshape(1, D),
        "affine_w": affine_w.reshape(T, D),
        "base": base.reshape(T, D),
        "pos": pos,
        "w_qkv": np.asarray(inputs["L0_attn_w_qkv"]),
        "w_out": np.asarray(inputs["L0_attn_w_out"]),
        "wg": np.asarray(inputs["L0_ffn_Wg"]).T,
        "w1": np.asarray(inputs["L0_ffn_W1"]).transpose(0, 2, 1),
        "w3": np.asarray(inputs["L0_ffn_W3"]).transpose(0, 2, 1),
        "w2": np.asarray(inputs["L0_ffn_W2"]).transpose(0, 2, 1),
    }
    nc = bacc.Bacc("TRN2", target_bir_lowering=False, num_devices=1)
    arrays, args = {}, []
    for name, a in data.items():
        a = np.ascontiguousarray(a)
        arrays[f"in_{name}"] = a
        args.append(nc.dram_tensor(f"in_{name}", a.shape, mybir.dt.from_np(a.dtype), kind="ExternalInput").ap())
    out = nc.dram_tensor("out", (BATCH, SEQ, D), F32, kind="ExternalOutput").ap()
    vit_tower(nc, *args, out)
    r = run_bass_kernel_spmd(nc, [arrays], core_ids=[0])
    return r.results[0]["out"]
```

```python
from contextlib import ExitStack

import concourse.bass as bass
from concourse import mybir

F32 = mybir.dt.float32
F32R = mybir.dt.float32r
BF16 = mybir.dt.bfloat16
I32 = mybir.dt.int32
U32 = mybir.dt.uint32
ALU = mybir.AluOpType
ACT = mybir.ActivationFunctionType
AX = mybir.AxisListType

P = 128
BATCH = 64
SEQ = 37
IMGS = 3
T = IMGS * SEQ
NT = -(-BATCH // IMGS)
TOKENS = BATCH * SEQ
LAST = TOKENS - (NT - 1) * T
D = 256
DC = D // P
PD = 768
PC = PD // P
HEADS = 16
HD = D // HEADS
HPC = P // HD
HB = 4
E = 8
CAP = TOKENS // E
HID = 512
HC = HID // P
EPS = 1e-5
ROW = D + E

J = P // E
F = TOKENS // J
FH = F // 2
LO = 16
HI = -(-CAP // LO)
ST = 3
SP_ = -(-CAP // ST)
HIGH_ROUNDS = 9
LOW_BITS = 31 - 2 * HIGH_ROUNDS
SEARCH = 15

C_ID = 0
C_MASK = C_ID + P
C_COS = C_MASK + T
C_SIN = C_COS + HD
C_HEAD = C_SIN + HD
C_E8 = C_HEAD + HPC
C_SCALE = C_E8 + E
C_BITS = C_SCALE + SEARCH + 1
C_FROW = C_BITS + 3 * (SEARCH + 1)
NC_F = C_FROW + 1
I_HI = 0
I_LO = I_HI + HI
I_U = I_LO + LO
I_BLOCK = I_U + 2 * P
I_TRI = I_BLOCK + P
NC_I = I_TRI + P

AV_EARLY = 7
EARLY_HEADS = [range(k * AV_EARLY // (PC - 2), (k + 1) * AV_EARLY // (PC - 2)) for k in range(PC - 2)]
ROPE = 3
STAGES = 4
NS = 4
NG = 3
NW = 2
PEELED = STAGES + 3
UNROLL = 3


class Tile:

    def __init__(self, i, slot, q):
        self.i, self.slot, self.q = i, slot, q


def run_steps(eng, step):
    def fixed(s):
        step([Tile(s - d, (s - d) % UNROLL, (s - d) // UNROLL) if 0 <= s - d < NT else None
              for d in range(STAGES + 1)])

    assert (NT - PEELED) % UNROLL == 0
    for s in range(PEELED):
        fixed(s)
    with eng.Fori(0, (NT - PEELED) // UNROLL) as j:
        for k in range(UNROLL):
            tiles = []
            for d in range(STAGES + 1):
                c = PEELED + k - d
                tiles.append(Tile(UNROLL * j + c, c % UNROLL, j + c // UNROLL))
            step(tiles)
    for s in range(NT, NT + STAGES):
        fixed(s)


def vit_tower(nc, x, consts, consts_i, ln1, lin_w, lin_b, affine_w, base, pos, w_qkv, w_out, wg, w1, w3, w2, out):
    ctx = ExitStack()
    with ctx:
        def sb(name, shape, dt=F32):
            return ctx.enter_context(nc.sbuf_tensor(name, shape, dt))

        def sem(name):
            return ctx.enter_context(nc.semaphore(name))

        def sems(name, n):
            return [sem(f"{name}{k}") for k in range(n)]

        def slots(name, shape, dt=F32, n=UNROLL):
            return [sb(f"{name}{k}", shape, dt) for k in range(n)]

        rows_dram = nc.dram_tensor("token_rows", (NT * T, ROW), F32, kind="Internal").ap()
        scores_dram = nc.dram_tensor("token_scores", (E, TOKENS), F32, kind="Internal").ap()
        ids_dram = nc.dram_tensor("slot_ids", (E, HI * LO), U32, kind="Internal").ap()

        cf = sb("cf", [P, NC_F])
        ci = sb("ci", [P, NC_I], I32)
        ident = cf[:, C_ID:C_ID + P]
        causal = cf[0:T, C_MASK:C_MASK + T]
        cos_t = cf[0:T, C_COS:C_COS + HD].unsqueeze(1).broadcast_to([T, 2 * HEADS, HD])
        sin_t = cf[0:T, C_SIN:C_SIN + HD]
        head_of = cf[:, C_HEAD:C_HEAD + HPC]
        expert_of = cf[:, C_E8:C_E8 + E]
        ln1_sb = sb("ln1_sb", [P, 2, PC])
        lin_sb = sb("lin_sb", [P, PC, D])
        linb_sb = sb("linb_sb", [T, D])
        affw_sb = sb("affw_sb", [T, D])
        base_sb = sb("base_sb", [T, D])
        pos_sb = sb("pos_sb", [T, D])
        wqkv_sb = sb("wqkv_sb", [P, DC, 3 * D])
        wqkv_hi = sb("wqkv_hi", [P, DC, 3 * D], F32R)
        wqkv_lo = sb("wqkv_lo", [P, DC, 3 * D], F32R)
        wout_sb = sb("wout_sb", [P, DC, D])
        wg_sb = sb("wg_sb", [P, DC, E])
        ones = sb("ones", [P, P])
        neg_half = sb("neg_half", [P, 1])

        scores = slots("scores", [E, T])
        w1_sb = slots("w1_sb", [P, DC, HID], n=NW)
        w3_sb = slots("w3_sb", [P, DC, HID], n=NW)
        w2_sb = slots("w2_sb", [P, HC, D], n=NW)

        lasting = ctx
        ctx = lasting.enter_context(ExitStack())
        x_in = slots("x_in", [T, PD])
        x_t = slots("x_t", [P, PC, T])
        y = slots("y", [T, D])
        h = slots("h", [T, D])
        xa = slots("xa", [T, D])
        xa_hi = slots("xa_hi", [P, DC, T], F32R)
        xa_lo = slots("xa_lo", [P, DC, T], F32R)
        qk = slots("qk", [T, 2 * D])
        v1 = slots("v1", [T, HEADS, HD + 1])
        rope_a = sb("rope_a", [T, 2 * D])
        rope_b = sb("rope_b", [T, 2 * D])
        qkr = slots("qkr", [T, 2 * D])
        expo = slots("expo", [T, 2 * D])
        feat = slots("feat", [T, 2 * D])
        k_t = slots("k_t", [P, DC, T])
        q_masked = sb("q_masked", [P, DC, HPC, T])
        s_t = slots("s_t", [T, HEADS, T])
        den = slots("den", [T, 2, HEADS])
        att = slots("att", [T, D])
        att_t = slots("att_t", [P, DC, T])
        h2 = slots("h2", [T, D])
        row = slots("row", [T, ROW])
        x2_t = slots("x2_t", [P, DC, T])
        stat = {n: slots(f"stat_{n}", [T, 12]) for n in ("ln1", "ln2", "ln3", "ln4")}
        mean_var = {n: slots(f"mv_{n}", [T, 2]) for n in ("ln1", "ln2", "ln3", "ln4")}
        var_eps = {n: slots(f"ve_{n}", [T, 1]) for n in ("ln1", "ln2", "ln3", "ln4")}
        rstd = {n: slots(f"rstd_{n}", [T, 1]) for n in ("ln1", "ln2", "ln3", "ln4")}

        ctx.close()
        ctx = lasting

        bank = [ctx.enter_context(nc.psum_tensor(f"bank{k}", [P, 512], F32)) for k in range(8)]
        S_BANKS = bank[0:3]
        B3, B4, B5, B6, B7 = bank[3:8]

        tables_loaded = sem("tables_loaded")
        lin_loaded = sem("lin_loaded")
        rows_loaded = sem("rows_loaded")
        w_qkv_loaded = sem("w_qkv_loaded")
        w_late_loaded = sem("w_late_loaded")
        setup = sem("setup")
        pool_ready = sem("pool_ready")
        x_loaded = sems("x_loaded", UNROLL)
        h2_stored = sems("h2_stored", UNROLL)
        row_stored = sems("row_stored", UNROLL)
        LN_STEPS = 4
        ln = {n: sem(f"dve_{n}") for n in ("ln1", "ln2", "ln3", "ln4")}
        rs = {n: sem(f"pool_{n}") for n in ("ln1", "ln2", "ln3", "ln4")}
        d_xt = sem("d_xt")
        w_split = sem("w_split")
        d_xat = sem("d_xat")
        d_kt = sem("d_kt")
        biased = sem("biased")
        affined = sem("affined")
        turned = sem("turned")
        roped = sem("roped")
        rectified = sem("rectified")
        feat_ready = sem("feat_ready")
        q_ready = sem("q_ready")
        s_masked = sem("s_masked")
        att_steps = sem("att_steps")
        h2_ready = sem("h2_ready")
        sc_copied = sem("sc_copied")
        pe_xt, pe_y, pe_xat, pe_qk, pe_v, pe_kt, pe_qt, pe_s, pe_av, pe_at, pe_o, pe_x2t, pe_sc, pe_sct = (
            sem(n) for n in ("pe_xt", "pe_y", "pe_xat", "pe_qk", "pe_v", "pe_kt", "pe_qt", "pe_s", "pe_av", "pe_at",
                             "pe_o", "pe_x2t", "pe_sc", "pe_sct"))
        a_xt, a_xat, a_qk, a_v, a_at, a_x2t, a_sct = (
            sem(n) for n in ("a_xt", "a_xat", "a_qk", "a_v", "a_at", "a_x2t", "a_sct"))
        N_CONST = 13

        w1_loaded, w3_loaded, w2_loaded = (sems(n, NW) for n in ("w1_loaded", "w3_loaded", "w2_loaded"))
        w1_high, w3_high, w2_high, w1_low, w3_low, w2_low = (
            sem(n) for n in ("w1_high", "w3_high", "w2_high", "w1_low", "w3_low", "w2_low"))
        sc128 = sb("sc128", [P, F])
        yv = sb("yv", [P, F])
        junk = sb("junk", [P, F])
        below = sb("below", [P, 3, F])
        sel_gt = sb("sel_gt", [P, F])
        sel_eq = sb("sel_eq", [P, F])
        scan = sb("scan", [P, F])
        picked = sb("picked", [P, F])
        ex = sb("ex", [P, F])
        zeros = sb("zeros", [P, F])
        cnt = sb("cnt", [P, 8], BF16)
        col = sb("col", [P, 16])
        part = sb("part", [P, 2, F], I32)
        high = sb("high", [P, F])
        low = sb("low", [P, F])
        rest = sb("rest", [P, F])
        cand = sb("cand", [P, 3])
        cand_part = sb("cand_part", [P, 3])
        junk3 = sb("junk3", [P, 3])
        block_ones = sb("block_ones", [P, P], BF16)
        block_tri = sb("block_tri", [P, P], BF16)
        diag_max = sb("diag_max", [P, P])
        max8 = sb("max8", [P, E])
        neg_max8 = sb("neg_max8", [P, E])
        e8 = sb("e8", [P, E])
        rz8 = sb("rz8", [P, E])
        slot_t = sb("slot_t", [FH, 2 * P], I32)
        hi_t = sb("hi_t", [FH, 2 * P], I32)
        lo_t = sb("lo_t", [FH, 2 * P], I32)
        hot_hi = slots("hot_hi", [FH, 2, J, HI], BF16, n=2)
        hot_lo = sb("hot_lo", [FH, 2, J, LO], BF16)
        hot_id = slots("hot_id", [FH, 2, J, 2, LO], BF16, n=2)
        u_bf = sb("u_bf", [FH, 2 * P], BF16)
        ids_bank = bank[0][0:HI, 512 - 2 * LO:512]
        id_f = sb("id_f", [HI, E, LO])
        id_u = sb("id_u", [HI, E, LO], U32)
        ids = sb("ids", [SP_, E, ST], U32)
        xg = slots("xg", [SP_, ST, ROW], n=NG)
        xg_hi = slots("xg_hi", [P, DC, CAP], F32R, n=2)
        xg_lo = slots("xg_lo", [P, DC, CAP], F32R, n=2)
        gate = slots("gate", [P, CAP], n=2)
        hid = slots("hid", [P, CAP], n=2)
        hid_hi = slots("hid_hi", [P, HC, CAP], F32R, n=2)
        hid_lo = slots("hid_lo", [P, HC, CAP], F32R, n=2)
        w1_hi = slots("w1_hi", [P, DC, HID], F32R, n=2)
        w1_lo = slots("w1_lo", [P, DC, HID], F32R, n=2)
        w3_hi = slots("w3_hi", [P, DC, HID], F32R, n=2)
        w3_lo = slots("w3_lo", [P, DC, HID], F32R, n=2)
        w2_hi = slots("w2_hi", [P, HC, D], F32R, n=2)
        w2_lo = slots("w2_lo", [P, HC, D], F32R, n=2)
        w_slot = slots("w_slot", [SP_, ST, 2], n=NS)
        y_w = slots("y_w", [SP_, ST, D], n=2)

        scores_out = sems("scores_out", UNROLL)
        scores_in = sem("scores_in")
        topk = sem("topk")
        pe_cnt = sem("pe_cnt")
        act_ex = sem("act_ex")
        hot_steps = sem("hot_steps")
        hot_ready = sem("hot_ready")
        pe_ids = sem("pe_ids")
        id_part = sem("id_part")
        ids_ready = sem("ids_ready")
        ids_out = sem("ids_out")
        ids_in = sems("ids_in", NG)
        gathered = sems("gathered", NG)
        scattered = sem("scattered")
        pe_xgt = sem("pe_xgt")
        a_xgt = sem("a_xgt")
        pe_h = sem("pe_h")
        a_gate = sem("a_gate")
        x_low = sem("x_low")
        hid_ready = sem("hid_ready")
        hid_high = sem("hid_high")
        hid_low = sem("hid_low")
        pe_y2 = sem("pe_y2")
        a_exp = sem("a_exp")
        w_ready = sem("w_ready")
        y_ready = sem("y_ready")

        def width(t):
            return LAST if isinstance(t.i, int) and t.i == NT - 1 else T

        def rows_of(dram, t, n):
            return dram[t.i * T:t.i * T + n, :] if isinstance(t.i, int) else dram[bass.ds(t.i * T, n), :]

        x_flat = x.rearrange("n t f -> (n t) f")
        out_flat = out.rearrange("b n d -> (b n) d")

        block = ctx.enter_context(nc.Block())

        @block.sync
        def _(sp):
            sp.dma_start(cf[:], consts).then_inc(tables_loaded, 16)

            def load_expert(e):
                w = e % NW
                if e >= NW:
                    sp.wait_ge(w1_low, e - NW + 1)
                    sp.wait_ge(w3_low, e - NW + 1)
                    sp.wait_ge(w2_low, e - NW + 1)
                sp.dma_start(w1_sb[w][:], w1[e].rearrange("(c p) h -> p c h", p=P)).then_inc(w1_loaded[w], 16)
                sp.dma_start(w3_sb[w][:], w3[e].rearrange("(c p) h -> p c h", p=P)).then_inc(w3_loaded[w], 16)
                sp.dma_start(w2_sb[w][:], w2[e].rearrange("(m p) d -> p m d", p=P)).then_inc(w2_loaded[w], 16)

            def step(tiles):
                t = tiles[0]
                if t:
                    if not isinstance(t.i, int) or t.i >= UNROLL:
                        sp.wait_ge(pe_xt, t.i - (UNROLL - 1))
                    sp.dma_start(x_in[t.slot][:], rows_of(x_flat, t, T)).then_inc(x_loaded[t.slot], 16)
                t = tiles[4]
                if t:
                    n = width(t)
                    o = (scores_dram[:, t.i * T:t.i * T + n] if isinstance(t.i, int)
                         else scores_dram[:, bass.ds(t.i * T, n)])
                    sp.wait_ge(h2_ready, t.i + 1)
                    sp.dma_start(rows_of(out_flat, t, n), h2[t.slot][0:n, :]).then_inc(h2_stored[t.slot], 16)
                    sp.wait_ge(a_sct, t.i + 1)
                    sp.dma_start(rows_of(rows_dram, t, T), row[t.slot][:]).then_inc(row_stored[t.slot], 16)
                    sp.dma_start(o, scores[t.slot][:, 0:n]).then_inc(scores_out[t.slot], 16)

            run_steps(sp, step)
            for k in range(UNROLL):
                sp.wait_ge(scores_out[k], 16 * len(range(k, NT, UNROLL)))
            sp.dma_start(sc128[:], scores_dram.rearrange("e (j f) -> (e j) f", j=J)).then_inc(scores_in, 16)
            for e in range(NW):
                load_expert(e)
            for e in range(E):
                sp.wait_ge(ids_ready, e + 1)
                sp.dma_start(ids_dram[e].rearrange("(hi lo) -> hi lo", lo=LO), id_u[:, e, :]).then_inc(ids_out, 16)
                sp.wait_ge(ids_out, 16 * (e + 1))
                sp.dma_start(ids[:, e, :],
                             ids_dram[e, 0:SP_ * ST].rearrange("(p s) -> p s", s=ST)).then_inc(ids_in[e % NG], 16)
                if e >= NW:
                    load_expert(e)

        @block.tensor
        def _(pe):
            pe.wait_ge(tables_loaded, 16)

            def turn(o, src, chunks, rows=T):
                for c in range(chunks):
                    mm = pe.transpose(o(c), src[:, c * P:(c + 1) * P], ident[0:rows, 0:rows])
                return mm

            def weigh_values(t, heads):
                for n in heads:
                    mm = pe.matmul(B6[0:T, n * (HD + 1):(n + 1) * (HD + 1)], s_t[t.slot][:, n, :],
                                   v1[t.slot][:, n, :], start=True, stop=True)
                return mm

            def project(o, t, cols):
                for c in range(DC):
                    pe.matmul(o, xa_hi[t.slot][:, c, :], wqkv_hi[:, c, cols], start=(c == 0), stop=False)
                    pe.matmul(o, xa_hi[t.slot][:, c, :], wqkv_lo[:, c, cols], start=False, stop=False)
                pe.wait_ge(d_xat, t.i + 1)
                for c in range(DC):
                    mm = pe.matmul(o, xa_lo[t.slot][:, c, :], wqkv_hi[:, c, cols], start=False, stop=(c == DC - 1))
                return mm

            def values_ready(t, former):
                pe.wait_ge(s_masked, 4 * t.i + 4)
                pe.wait_ge(a_v, t.i + 1)
                if former:
                    pe.wait_ge(sc_copied, t.i)

            def score(t, b):
                g, c = b // 2, b % 2
                if b == 0:
                    pe.wait_ge(d_kt, t.i + 1)
                pe.wait_ge(q_ready, 2 * t.i + g + 1)
                if b >= len(S_BANKS):
                    pe.wait_ge(s_masked, 4 * t.i + b - len(S_BANKS) + 1)
                pe.matmul(S_BANKS[b % len(S_BANKS)][0:T, 0:HB * T], k_t[t.slot][:, c, :],
                          q_masked[:, c, g * HB:(g + 1) * HB, :], start=True, stop=True).then_inc(pe_s, 1)

            def step(tiles):
                t0, t1, t2, t3, t4 = tiles
                if t1:
                    pe.wait_ge(d_xt, t1.i + 1)
                    if isinstance(t1.i, int) and t1.i == 0:
                        pe.wait_ge(lin_loaded, 32)
                    else:
                        pe.wait_ge(a_qk, t1.i)
                    for k in range(PC):
                        if k == PC // 2:
                            pe.wait_ge(a_xt, t1.i + 1)
                        c = (k + PC // 2) % PC
                        mm = pe.matmul(B7[0:T, 0:D], x_t[t1.slot][:, c, :], lin_sb[:, c, :],
                                       start=(k == 0), stop=(k == PC - 1))
                        if t3 and k == 1:
                            values_ready(t3, t4)
                        if t3 and 1 <= k < PC - 1:
                            weigh_values(t3, EARLY_HEADS[k - 1])
                    mm.then_inc(pe_y, 1)
                elif t3:
                    values_ready(t3, t4)
                    weigh_values(t3, range(0, AV_EARLY))
                if t2:
                    pe.wait_ge(feat_ready, t2.i + 1)
                    turn(lambda c: B4[:, c * T:(c + 1) * T], feat[t2.slot][:, D:], DC).then_inc(pe_kt, 1)
                    turn(lambda c: B5[:, c * T:(c + 1) * T], feat[t2.slot], DC).then_inc(pe_qt, 1)
                if t3:
                    weigh_values(t3, range(AV_EARLY, HEADS)).then_inc(pe_av, 1)
                if t2:
                    score(t2, 0)
                    score(t2, 1)
                if t3:
                    pe.wait_ge(att_steps, 3 * t3.i + 3)
                    turn(lambda c: B4[:, c * T:(c + 1) * T], att[t3.slot], DC).then_inc(pe_at, 1)
                if t4:
                    pe.wait_ge(sc_copied, t4.i + 1)
                    pe.transpose(B4[0:E, DC * T:(DC + 1) * T], row[t4.slot][:, D:ROW],
                                 ident[0:T, 0:T]).then_inc(pe_sct, 1)
                if t2:
                    score(t2, 2)
                if t3:
                    if isinstance(t3.i, int) and t3.i == 0:
                        pe.wait_ge(w_late_loaded, 48)
                    pe.wait_ge(a_at, t3.i + 1)
                    for c in range(DC):
                        mm = pe.matmul(B6[0:T, 0:D], att_t[t3.slot][:, c, :], wout_sb[:, c, :],
                                       start=(c == 0), stop=(c == DC - 1))
                    mm.then_inc(pe_o, 1)
                if t1:
                    pe.wait_ge(ln["ln3"], LN_STEPS * t1.i + 4)
                    if t2:
                        pe.wait_ge(q_ready, 2 * t2.i + 2)
                    turn(lambda c: B5[:, c * T:(c + 1) * T], xa[t1.slot], DC).then_inc(pe_xat, 1)
                if t2:
                    score(t2, 3)
                if t1:
                    if isinstance(t1.i, int) and t1.i == 0:
                        pe.wait_ge(w_split, 2)
                    pe.wait_ge(a_xat, t1.i + 1)
                    project(B7[0:T, 0:2 * D], t1, slice(0, 2 * D)).then_inc(pe_qk, 1)
                if t0:
                    pe.wait_ge(ln["ln1"], LN_STEPS * t0.i + 4)
                    if t4:
                        pe.wait_ge(a_sct, t4.i + 1)
                    turn(lambda c: (B4 if c < PC // 2 else B5)[:, c % (PC // 2) * T:(c % (PC // 2) + 1) * T],
                         x_in[t0.slot], PC).then_inc(pe_xt, 1)
                if t3:
                    pe.wait_ge(ln["ln4"], LN_STEPS * t3.i + 4)
                    turn(lambda c: B6[:, D + c * T:D + (c + 1) * T], row[t3.slot], DC).then_inc(pe_x2t, 1)
                if t1:
                    project(B3[0:T, 0:D], t1, slice(2 * D, 3 * D)).then_inc(pe_v, 1)
                if t3:
                    pe.wait_ge(a_x2t, t3.i + 1)
                    for c in range(DC):
                        mm = pe.matmul(B6[0:T, 0:E], x2_t[t3.slot][:, c, :], wg_sb[:, c, :],
                                       start=(c == 0), stop=(c == DC - 1))
                    mm.then_inc(pe_sc, 1)

            run_steps(pe, step)

            def count(lhs, rhs, o, dve_at):
                pe.wait_ge(topk, dve_at)
                pe.matmul(o, lhs, rhs, start=True, stop=True).then_inc(pe_cnt, 1)

            pe.wait_ge(sc_copied, NT)
            pe.wait_ge(a_sct, NT)
            pe.wait_ge(a_v, NT)
            count(block_ones[:], cnt[:, 0:1], B7[:, 0:1], TK_SIGN)
            count(ones[:], diag_max[:], B6[:, 0:P], TK_MAX)
            with pe.Fori(0, HIGH_ROUNDS // 3) as r:
                for k in range(3):
                    count(block_ones[:], cnt[:, 1:4], B7[:, 0:3], TK_SEARCH + TK_ROUND * (3 * r + k) + 2)
            with pe.Fori(0, (SEARCH - HIGH_ROUNDS) // 3) as r:
                for k in range(3):
                    count(block_ones[:], cnt[:, 1:4], B7[:, 0:3],
                          TK_SEARCH + 3 + TK_ROUND * (3 * r + HIGH_ROUNDS + k) + 2)
            count(block_ones[:], cnt[:, 1:2], B7[:, 0:1], TK_LAST + 2)
            pe.wait_ge(topk, TK_GT)
            pe.matmul(B7[:, 0:1], block_ones[:], cnt[:, 4:5], start=True, stop=True)
            pe.matmul(B7[:, 1:2], block_tri[:], cnt[:, 5:6], start=True, stop=True).then_inc(pe_cnt, 1)
            count(block_tri[:], cnt[:, 6:7], B7[:, 0:1], TK_SEL)
            pe.wait_ge(topk, TK_POS)
            for c in range(2):
                mm = pe.transpose(B4[0:FH, c * P:(c + 1) * P], picked[:, c * FH:(c + 1) * FH], ident)
            mm.then_inc(pe_cnt, 1)

            def listing(e):
                pe.wait_ge(hot_ready, e + 1)
                for n in range(2 * J):
                    mm = pe.matmul(ids_bank, hot_hi[e % 2][:, n // J, n % J, :], hot_id[e % 2][:, n // J, n % J, :, :],
                                   start=(n == 0), stop=(n == 2 * J - 1))
                mm.then_inc(pe_ids, 1)

            listing(0)
            count(ones[:], e8[:], B6[:, 0:E], TK_Z)
            pe.wait_ge(ids_ready, 1)
            listing(1)
            pe.wait_ge(ids_ready, 2)
            listing(2)

            def up(e):
                pe.wait_ge(gathered[e % NG], 16 * ST * (e // NG + 1))
                if e >= 1:
                    pe.wait_ge(x_low, DC * e)
                pe.wait_ge(ids_ready, min(e + 3, E))
                for c in range(DC):
                    for s in range(ST):
                        n = min(SP_, CAP - s * SP_)
                        mm = pe.transpose(bank[c][:, s * SP_:s * SP_ + n], xg[e % NG][0:n, s, c * P:(c + 1) * P],
                                          ident[0:n, 0:n])
                    mm.then_inc(pe_xgt, 1)

            def hidden(e, m):
                k = HC * e + m
                if m == 0:
                    pe.wait_ge(a_xgt, DC * (e + 1))
                    pe.wait_ge(x_low, DC * (e + 1))
                    pe.wait_ge(w1_high, e + 1)
                    pe.wait_ge(w1_low, e + 1)
                if k >= 2:
                    pe.wait_ge(hid_ready, k - 1)
                w = e % 2
                for which, (o, hi, lo) in enumerate(((bank[2 + 2 * (k % 2)], w1_hi[w], w1_lo[w]),
                                                     (bank[3 + 2 * (k % 2)], w3_hi[w], w3_lo[w]))):
                    if m == 0 and which == 1:
                        pe.wait_ge(w3_high, e + 1)
                        pe.wait_ge(w3_low, e + 1)
                    for c in range(DC):
                        h_cols = slice(m * P, (m + 1) * P)
                        pe.matmul(o[:, 0:CAP], hi[:, c, h_cols], xg_hi[w][:, c, :], start=(c == 0), stop=False)
                        pe.matmul(o[:, 0:CAP], hi[:, c, h_cols], xg_lo[w][:, c, :], start=False, stop=False)
                        mm = pe.matmul(o[:, 0:CAP], lo[:, c, h_cols], xg_hi[w][:, c, :], start=False,
                                       stop=(c == DC - 1))
                mm.then_inc(pe_h, 1)

            def down(e):
                pe.wait_ge(w2_high, e + 1)
                pe.wait_ge(w2_low, e + 1)
                w = e % 2
                for s in range(ST):
                    n = min(SP_, CAP - s * SP_)
                    k = ST * e + s
                    if k >= 2:
                        pe.wait_ge(y_ready, k - 1)
                    o = bank[6 + k % 2][0:n, 0:D]
                    for m in range(HC):
                        rows = slice(s * SP_, s * SP_ + n)
                        if s == 0:
                            pe.wait_ge(hid_high, HC * e + m + 1)
                            pe.wait_ge(hid_low, HC * e + m + 1)
                        pe.matmul(o, hid_hi[w][:, m, rows], w2_hi[w][:, m, :], start=(m == 0), stop=False)
                        pe.matmul(o, hid_hi[w][:, m, rows], w2_lo[w][:, m, :], start=False, stop=False)
                        mm = pe.matmul(o, hid_lo[w][:, m, rows], w2_hi[w][:, m, :], start=False,
                                       stop=(m == HC - 1))
                    mm.then_inc(pe_y2, 1)

            up(0)
            hidden(0, 0)
            for e in range(E):
                hidden(e, 1)
                if e + NG < E:
                    listing(e + NG)
                hidden(e, 2)
                if e + 1 < E:
                    up(e + 1)
                hidden(e, 3)
                if e + 1 < E:
                    hidden(e + 1, 0)
                down(e)

        @block.scalar
        def _(act):
            act.dma_start(ln1_sb[:], ln1).then_inc(lin_loaded, 16)
            act.dma_start(lin_sb[:], lin_w.rearrange("(c p) d -> p c d", p=P)).then_inc(lin_loaded, 16)
            act.dma_start(linb_sb[:], lin_b).then_inc(rows_loaded, 16)
            act.dma_start(affw_sb[:], affine_w).then_inc(rows_loaded, 16)
            act.dma_start(base_sb[:], base).then_inc(rows_loaded, 16)
            act.dma_start(pos_sb[:], pos).then_inc(rows_loaded, 16)
            act.dma_start(wqkv_sb[:], w_qkv.rearrange("(c p) d -> p c d", p=P)).then_inc(w_qkv_loaded, 16)
            act.dma_start(wout_sb[:], w_out.rearrange("(c p) d -> p c d", p=P)).then_inc(w_late_loaded, 16)
            act.dma_start(wg_sb[:], wg.rearrange("(c p) e -> p c e", p=P)).then_inc(w_late_loaded, 16)
            act.dma_start(ci[:], consts_i).then_inc(w_late_loaded, 16)

            def patches(t, c):
                return nc.scalar.activation(x_t[t.slot][:, c, :], B4[:, c * T:(c + 1) * T], ACT.Identity,
                                            bias=ln1_sb[:, 1, c:c + 1], scale=ln1_sb[:, 0, c:c + 1])

            def queries(t, n):
                return nc.scalar.activation(q_masked[:, :, n, :],
                                            B5[:, 0:DC * T].rearrange("p (c t) -> p c t", c=DC), ACT.Copy,
                                            scale=head_of[:, n:n + 1])

            def step(tiles):
                t0, t1, t2, t3, t4 = tiles
                if t2:
                    act.wait_ge(roped, ROPE * t2.i + ROPE)
                    nc.scalar.activation(expo[t2.slot][:], qkr[t2.slot][:], ACT.Exp)
                    nc.scalar.activation(qkr[t2.slot][:], qkr[t2.slot][:], ACT.Relu).then_inc(rectified, 1)
                    act.wait_ge(pe_qt, t2.i + 1)
                    for g in range(2):
                        for n in range(g * HB, (g + 1) * HB):
                            last = queries(t2, n)
                        last.then_inc(q_ready, 1)
                if t3:
                    act.wait_ge(pe_at, t3.i + 1)
                    if t4:
                        act.wait_ge(pe_sct, t4.i + 1)
                    nc.scalar.copy(att_t[t3.slot][:], B4[:, 0:DC * T]).then_inc(a_at, 1)
                if t4:
                    act.wait_ge(pe_sct, t4.i + 1)
                    if not isinstance(t4.i, int) or t4.i >= UNROLL:
                        act.wait_ge(scores_out[t4.slot], 16 * t4.q)
                    nc.scalar.copy(scores[t4.slot][:], B4[0:E, DC * T:(DC + 1) * T]).then_inc(a_sct, 1)
                if t1:
                    act.wait_ge(pe_xat, t1.i + 1)
                    nc.scalar.copy(xa_hi[t1.slot][:], B5[:, 0:DC * T]).then_inc(a_xat, 1)
                    act.wait_ge(pe_qk, t1.i + 1)
                    nc.scalar.copy(qk[t1.slot][:], B7[0:T, 0:2 * D]).then_inc(a_qk, 1)
                if t0:
                    act.wait_ge(pe_xt, t0.i + 1)
                    patches(t0, 0)
                if t3:
                    act.wait_ge(pe_x2t, t3.i + 1)
                    nc.scalar.copy(x2_t[t3.slot][:], B6[:, D:D + DC * T]).then_inc(a_x2t, 1)
                if t0:
                    for c in range(1, PC // 2):
                        last = patches(t0, c)
                    last.then_inc(a_xt, 1)
                if t1:
                    act.wait_ge(pe_v, t1.i + 1)
                    nc.scalar.copy(v1[t1.slot][:, :, 0:HD],
                                   B3[0:T, 0:D].rearrange("t (n d) -> t n d", n=HEADS)).then_inc(a_v, 1)

            act.wait_ge(setup, 1)
            act.wait_ge(tables_loaded, 16)
            act.wait_ge(lin_loaded, 32)
            act.wait_ge(w_qkv_loaded, 16)
            nc.scalar.copy(wqkv_hi[:], wqkv_sb[:]).then_inc(w_split, 1)
            run_steps(act, step)

            def turned_high(e):
                for c in range(DC):
                    act.wait_ge(pe_xgt, DC * e + c + 1)
                    if c == 0 and e >= 2:
                        act.wait_ge(pe_h, HC * (e - 1))
                    nc.scalar.copy(xg_hi[e % 2][:, c, :], bank[c][:, 0:CAP]).then_inc(a_xgt, 1)

            def open_gate(e, m):
                k = HC * e + m
                act.wait_ge(pe_h, k + 1)
                if k >= 2:
                    act.wait_ge(hid_ready, k - 1)
                nc.scalar.activation(gate[k % 2][:], bank[2 + 2 * (k % 2)][:, 0:CAP], ACT.Silu).then_inc(a_gate, 1)

            def hidden_high(e, m):
                act.wait_ge(hid_ready, HC * e + m + 1)
                if m == 0 and e >= 2:
                    act.wait_ge(pe_y2, ST * (e - 1))
                nc.scalar.copy(hid_hi[e % 2][:, m, :], hid[m % 2][:]).then_inc(hid_high, 1)

            def exponentials(e):
                act.wait_ge(gathered[e % NG], 16 * ST * (e // NG + 1))
                if e >= NS:
                    act.wait_ge(y_ready, ST * (e - NS + 1))
                for s in range(ST):
                    n = min(SP_, CAP - s * SP_)
                    last = nc.scalar.activation(w_slot[e % NS][0:n, s, 0:1], xg[e % NG][0:n, s, D + e:D + e + 1],
                                                ACT.Exp, bias=neg_max8[0:n, e:e + 1])
                last.then_inc(a_exp, 1)

            def weight_high(e, raw, hi, loaded, done, used):
                act.wait_ge(loaded[e % NW], 16 * (e // NW + 1))
                if e >= 2:
                    act.wait_ge(*used)
                nc.scalar.copy(hi[e % 2][:], raw[e % NW][:]).then_inc(done, 1)

            def w1_split(e):
                weight_high(e, w1_sb, w1_hi, w1_loaded, w1_high, (pe_h, HC * (e - 1)))

            def w3_split(e):
                weight_high(e, w3_sb, w3_hi, w3_loaded, w3_high, (pe_h, HC * (e - 1)))

            def w2_split(e):
                weight_high(e, w2_sb, w2_hi, w2_loaded, w2_high, (pe_y2, ST * (e - 1)))

            w1_split(0)
            w3_split(0)
            w2_split(0)
            w1_split(1)
            w3_split(1)
            act.wait_ge(topk, TK_MAXOWN)
            nc.scalar.activation(ex[:], sc128[:], ACT.Exp, bias=col[:, 5:6]).then_inc(act_ex, 1)

            exponentials(0)
            turned_high(0)
            open_gate(0, 0)
            hidden_high(0, 0)
            for e in range(E):
                open_gate(e, 1)
                hidden_high(e, 1)
                if e + 1 < E:
                    w2_split(e + 1)
                open_gate(e, 2)
                if e + 1 < E:
                    turned_high(e + 1)
                hidden_high(e, 2)
                open_gate(e, 3)
                if e + 2 < E:
                    w1_split(e + 2)
                hidden_high(e, 3)
                if e + 1 < E:
                    open_gate(e + 1, 0)
                    hidden_high(e + 1, 0)
                    if e % 2 == 0:
                        for k in range(e + 1, min(e + 3, E)):
                            exponentials(k)
                if e + 2 < E:
                    w3_split(e + 2)

        @block.vector
        def _(dve):
            V = nc.vector
            V.memset(ones[:], 1.0)
            for k in range(UNROLL):
                V.memset(v1[k][:], 1.0)
            V.memset(neg_half[:], -0.5).then_inc(setup, 1)

            def ln_stats(n, t, src, width, meanwhile=None):
                parts = -(-width // 512)
                w = width // parts
                for k in range(parts):
                    last = V.bn_stats(stat[n][t.slot][:, 6 * k:6 * k + 6], src[:, k * w:(k + 1) * w])
                last.then_inc(ln[n], 1)
                if meanwhile:
                    meanwhile()
                dve.wait_ge(ln[n], LN_STEPS * t.i + 1)
                V.memset(var_eps[n][t.slot][:], EPS)
                V.bn_aggr(mean_var[n][t.slot][:], stat[n][t.slot][:, 0:6 * parts]).then_inc(ln[n], 1)
                dve.wait_ge(ln[n], LN_STEPS * t.i + 2)
                V.tensor_tensor(var_eps[n][t.slot][:], var_eps[n][t.slot][:], mean_var[n][t.slot][:, 1:2],
                                ALU.add).then_inc(ln[n], 1)

            def ln_scale(n, t, dst, src):
                dve.wait_ge(rs[n], t.i + 1)
                V.tensor_scalar(dst, src, mean_var[n][t.slot][:, 0:1], rstd[n][t.slot][:], ALU.subtract,
                                ALU.mult).then_inc(ln[n], 1)

            def mask_scores(t, b):
                g, c = b // 2, b % 2
                n = c * HPC + g * HB
                dve.wait_ge(pe_s, 4 * t.i + b + 1)
                V.tensor_tensor(s_t[t.slot][:, n:n + HB, :],
                                S_BANKS[b % len(S_BANKS)][0:T, 0:HB * T].rearrange("s (n t) -> s n t", n=HB),
                                causal.unsqueeze(1).broadcast_to([T, HB, T]), ALU.mult).then_inc(s_masked, 1)

            def turned_low(t):
                dve.wait_ge(a_xat, t.i + 1)
                V.tensor_tensor(xa_lo[t.slot][:], B5[:, 0:DC * T].rearrange("p (c t) -> p c t", c=DC),
                                xa_hi[t.slot][:].bitcast(F32), ALU.subtract).then_inc(d_xat, 1)

            def step(tiles):
                t0, t1, t2, t3, t4 = tiles
                if t0:
                    dve.wait_ge(x_loaded[t0.slot], 16 * t0.q + 16)
                    ln_stats("ln1", t0, x_in[t0.slot], PD)
                if t0:
                    ln_scale("ln1", t0, x_in[t0.slot][:], x_in[t0.slot][:])
                if t2:
                    dve.wait_ge(rectified, t2.i + 1)
                    V.scalar_tensor_tensor(out=feat[t2.slot][:], in0=expo[t2.slot][:], scalar=1.0,
                                           in1=qkr[t2.slot][:], op0=ALU.min, op1=ALU.add).then_inc(feat_ready, 1)
                if t1:
                    if isinstance(t1.i, int) and t1.i == 0:
                        dve.wait_ge(rows_loaded, 64)
                        V.tensor_tensor(base_sb[:], base_sb[:], pos_sb[:], ALU.add)
                        dve.wait_ge(w_split, 1)
                        V.tensor_tensor(wqkv_lo[:], wqkv_sb[:], wqkv_hi[:].bitcast(F32),
                                        ALU.subtract).then_inc(w_split, 1)
                    dve.wait_ge(pe_y, t1.i + 1)
                    V.tensor_tensor(y[t1.slot][:], B7[0:T, 0:D], linb_sb[:], ALU.add).then_inc(biased, 1)
                if t2:
                    dve.wait_ge(pe_kt, t2.i + 1)
                    V.tensor_copy(k_t[t2.slot][:], B4[:, 0:DC * T]).then_inc(d_kt, 1)
                if t1:
                    dve.wait_ge(biased, t1.i + 1)
                    ln_stats("ln2", t1, y[t1.slot], D)
                    V.scalar_tensor_tensor(out=y[t1.slot][:], in0=y[t1.slot][:],
                                           scalar=mean_var["ln2"][t1.slot][:, 0:1], in1=affw_sb[:],
                                           op0=ALU.subtract, op1=ALU.mult).then_inc(ln["ln2"], 1)
                if t3:
                    dve.wait_ge(pe_av, t3.i + 1)
                    o = B6[0:T, 0:HEADS * (HD + 1)].rearrange("t (n d) -> t n d", n=HEADS)
                    V.tensor_scalar(den[t3.slot][:, 0, :], o[:, :, HD], 1e-6, None, ALU.max).then_inc(att_steps, 1)
                    dve.wait_ge(att_steps, 3 * t3.i + 1)
                    V.reciprocal(den[t3.slot][:, 1, :], den[t3.slot][:, 0, :]).then_inc(att_steps, 1)
                    dve.wait_ge(att_steps, 3 * t3.i + 2)
                    V.tensor_tensor(att[t3.slot][:].rearrange("t (n d) -> t n d", n=HEADS), o[:, :, 0:HD],
                                    den[t3.slot][:, 1, :].unsqueeze(2).broadcast_to([T, HEADS, HD]),
                                    ALU.mult).then_inc(att_steps, 1)
                if t1:
                    dve.wait_ge(rs["ln2"], t1.i + 1)
                    dve.wait_ge(ln["ln2"], LN_STEPS * t1.i + 4)
                    V.scalar_tensor_tensor(out=h[t1.slot][:], in0=y[t1.slot][:], scalar=rstd["ln2"][t1.slot][:],
                                           in1=base_sb[:], op0=ALU.mult, op1=ALU.add).then_inc(affined, 1)
                    dve.wait_ge(affined, t1.i + 1)
                    ln_stats("ln3", t1, h[t1.slot], D)
                if t2:
                    mask_scores(t2, 0)
                if t1:
                    ln_scale("ln3", t1, xa[t1.slot][:], h[t1.slot][:])
                if t2:
                    mask_scores(t2, 1)
                if t3:
                    dve.wait_ge(pe_o, t3.i + 1)
                    if not isinstance(t3.i, int) or t3.i >= UNROLL:
                        dve.wait_ge(h2_stored[t3.slot], 16 * t3.q)
                        dve.wait_ge(row_stored[t3.slot], 16 * t3.q)
                    V.tensor_tensor(h2[t3.slot][:], B6[0:T, 0:D], h[t3.slot][:], ALU.add).then_inc(h2_ready, 1)
                    dve.wait_ge(h2_ready, t3.i + 1)
                    ln_stats("ln4", t3, h2[t3.slot], D, (lambda: turned_low(t1)) if t1 else None)
                elif t1:
                    turned_low(t1)
                if t2:
                    mask_scores(t2, 2)
                if t3:
                    ln_scale("ln4", t3, row[t3.slot][:, 0:D], h2[t3.slot][:])
                if t0:
                    dve.wait_ge(pe_xt, t0.i + 1)
                    for c in range(PC // 2, PC):
                        last = V.tensor_scalar(x_t[t0.slot][:, c, :], B5[:, (c - PC // 2) * T:(c - PC // 2 + 1) * T],
                                               ln1_sb[:, 0, c:c + 1], ln1_sb[:, 1, c:c + 1], ALU.mult, ALU.add)
                    last.then_inc(d_xt, 1)
                if t2:
                    mask_scores(t2, 3)
                if t1:
                    dve.wait_ge(a_qk, t1.i + 1)
                    if not isinstance(t1.i, int) or t1.i >= 1:
                        dve.wait_ge(roped, ROPE * t1.i)
                    V.tensor_tensor(rope_a[:].rearrange("t (n d) -> t n d", d=HD),
                                    qk[t1.slot][:].rearrange("t (n d) -> t n d", d=HD), cos_t,
                                    ALU.mult).then_inc(turned, 1)
                if t3:
                    dve.wait_ge(pe_sc, t3.i + 1)
                    V.tensor_copy(row[t3.slot][:, D:ROW], B6[0:T, 0:E]).then_inc(sc_copied, 1)

            dve.wait_ge(tables_loaded, 16)
            dve.wait_ge(lin_loaded, 32)
            run_steps(dve, step)
            dve.wait_ge(w_late_loaded, 48)

            at = [0]

            def link(ins):
                at[0] += 1
                ins.then_inc(topk, 1)
                dve.wait_ge(topk, at[0])

            def mark(name):
                assert at[0] == name, (at[0], name)

            sgn, lim, t_s, need, g_max, nmax_own, new_bits, zc, soff, eoff, thr = (col[:, k:k + 1] for k in range(11))
            for k in range(UNROLL):
                n = len(range(k, NT, UNROLL))
                dve.wait_ge(h2_stored[k], 16 * n)
                dve.wait_ge(row_stored[k], 16 * n)
            V.memset(zeros[:], 0.0)
            V.memset(col[:], 0.0)
            V.tensor_copy(cand_part[:], cf[:, C_BITS:C_BITS + 3])
            V.tensor_copy(block_ones[:], ci[:, I_BLOCK:I_BLOCK + P])
            V.tensor_copy(block_tri[:], ci[:, I_TRI:I_TRI + P])
            V.tensor_copy(u_bf[:], ci[0:FH, I_U:I_U + 2 * P])
            dve.wait_ge(scores_in, 16)
            link(V.tensor_scalar(junk[:], sc128[:], 0.0, None, ALU.is_ge, ALU.add, accum_out=cnt[:, 0:1]))
            mark(TK_SIGN)
            link(V.reduce_max(g_max, sc128[:], AX.X))
            link(V.tensor_scalar(diag_max[:], ident, g_max, None, ALU.mult))
            mark(TK_MAX)
            dve.wait_ge(pe_cnt, 1)
            link(V.tensor_scalar(lim, B7[:, 0:1], float(CAP), 2.0, ALU.is_ge, ALU.mult))
            link(V.tensor_scalar(sgn, lim, -1.0, None, ALU.add))
            link(V.tensor_scalar(lim, sgn, (TOKENS - 2 * CAP + 1) / 2, (TOKENS - 1) / 2, ALU.mult, ALU.add))
            link(V.tensor_scalar(yv[:], sc128[:], sgn, 0.0, ALU.mult, ALU.add))
            V.tensor_scalar(part[:, 0, :], yv[:].bitcast(I32), LOW_BITS, None, ALU.arith_shift_right)
            link(V.tensor_scalar(part[:, 1, :], yv[:].bitcast(I32), (1 << LOW_BITS) - 1, None, ALU.bitwise_and))
            V.tensor_copy(high[:], part[:, 0, :])
            link(V.tensor_copy(low[:], part[:, 1, :]))
            dve.wait_ge(pe_cnt, 2)
            link(V.reduce_max(max8[:], B6[:, 0:P].rearrange("p (e j) -> p e j", e=E), AX.X))
            link(V.tensor_scalar(neg_max8[:], max8[:], -1.0, None, ALU.mult))
            link(V.tensor_tensor(e8[:], neg_max8[:], expert_of, ALU.mult))
            link(V.reduce_sum(nmax_own, e8[:], AX.X))
            mark(TK_MAXOWN)
            mark(TK_SEARCH)

            def search(src, tab_next, scale, n, k, pe_k):
                V.tensor_tensor(cand[:, 0:n], cand_part[:, 0:n], new_bits.broadcast_to([P, n]),
                                ALU.add).then_inc(topk, 1)
                dve.wait_ge(topk, k + 1)
                for c in range(n):
                    last = V.tensor_scalar(below[:, c, :], src[:], cand[:, c:c + 1], None, ALU.is_lt,
                                           ALU.add, accum_out=cnt[:, 1 + c:2 + c])
                last.then_inc(topk, 1)
                V.tensor_tensor(thr, thr, new_bits, ALU.add).then_inc(topk, 1)
                dve.wait_ge(topk, k + 3)
                V.tensor_tensor(cand_part[:], thr.broadcast_to([P, 3]), tab_next, ALU.add).then_inc(topk, 1)
                dve.wait_ge(pe_cnt, pe_k)
                dve.wait_ge(topk, k + 4)
                V.scalar_tensor_tensor(out=junk3[:, 0:n], in0=B7[:, 0:n], scalar=lim,
                                       in1=scale.broadcast_to([P, n]), op0=ALU.is_le, op1=ALU.mult,
                                       accum_out=new_bits).then_inc(topk, 1)
                dve.wait_ge(topk, k + 5)

            def rounds(src, first, n, k0):
                with dve.Fori(0, n // 3) as r:
                    for k in range(3):
                        q = 3 * r + (first + k)
                        search(src, cf[:, bass.ds(3 * q + C_BITS + 3, 3)], cf[:, bass.ds(q + C_SCALE, 1)], 3,
                               TK_ROUND * q + k0, q + 3)

            rounds(high, 0, HIGH_ROUNDS, TK_SEARCH)
            at[0] = TK_SEARCH + TK_ROUND * HIGH_ROUNDS
            link(V.tensor_tensor(thr, thr, new_bits, ALU.add))
            link(V.tensor_scalar(high[:], high[:], thr, float(1 << LOW_BITS), ALU.subtract, ALU.mult))
            V.tensor_tensor(rest[:], high[:], low[:], ALU.add)
            V.memset(thr, 0.0)
            V.memset(new_bits, 0.0)
            link(V.tensor_copy(cand_part[:], cf[:, C_BITS + 3 * HIGH_ROUNDS:C_BITS + 3 * HIGH_ROUNDS + 3]))
            rounds(rest, HIGH_ROUNDS, SEARCH - HIGH_ROUNDS, TK_SEARCH + 3)
            search(rest, cf[:, C_BITS:C_BITS + 3], cf[:, C_SCALE + SEARCH:C_SCALE + SEARCH + 1], 1, TK_LAST,
                   3 + SEARCH)
            at[0] = TK_LAST + TK_ROUND
            n_pe = 3 + SEARCH
            link(V.tensor_tensor(thr, thr, new_bits, ALU.add))
            V.tensor_scalar(rest[:], rest[:], sgn, None, ALU.mult)
            link(V.tensor_scalar(t_s, thr, sgn, None, ALU.mult))
            V.tensor_scalar(sel_gt[:], rest[:], t_s, None, ALU.is_gt, ALU.add, accum_out=cnt[:, 4:5])
            link(V.tensor_scalar(sel_eq[:], rest[:], t_s, None, ALU.is_equal, ALU.add, accum_out=cnt[:, 5:6]))
            mark(TK_GT)
            dve.wait_ge(pe_cnt, n_pe + 1)
            V.tensor_copy(eoff, B7[:, 1:2])
            link(V.tensor_scalar(need, B7[:, 0:1], -1.0, float(CAP), ALU.mult, ALU.add))
            link(V.tensor_tensor_scan(scan[:], sel_eq[:], zeros[:], eoff, ALU.add, ALU.add))
            link(V.scalar_tensor_tensor(out=junk[:], in0=scan[:], scalar=need, in1=sel_eq[:], op0=ALU.is_le,
                                        op1=ALU.mult))
            link(V.scalar_tensor_tensor(out=picked[:], in0=junk[:], scalar=0.0, in1=sel_gt[:], op0=ALU.add,
                                        op1=ALU.add, accum_out=cnt[:, 6:7]))
            mark(TK_SEL)
            dve.wait_ge(act_ex, 1)
            V.scalar_tensor_tensor(out=junk[:], in0=ex[:], scalar=1.0, in1=picked[:], op0=ALU.mult,
                                   op1=ALU.mult, accum_out=zc)
            dve.wait_ge(pe_cnt, n_pe + 2)
            link(V.tensor_copy(soff, B7[:, 0:1]))
            link(V.tensor_tensor_scan(scan[:], picked[:], zeros[:], soff, ALU.add, ALU.add))
            link(V.tensor_tensor(picked[:], picked[:], scan[:], ALU.mult))
            mark(TK_POS)
            link(V.tensor_scalar(e8[:], expert_of, zc, None, ALU.mult))
            mark(TK_Z)
            dve.wait_ge(pe_cnt, n_pe + 3)
            link(V.tensor_scalar(slot_t[:], B4[0:FH, 0:2 * P], -1.0, None, ALU.add))
            V.tensor_scalar(hi_t[:], slot_t[:], 4, None, ALU.arith_shift_right)
            link(V.tensor_scalar(lo_t[:], slot_t[:], LO - 1, None, ALU.bitwise_and))
            mark(TK_SLOT)

            def by_expert(a, e):
                return a.rearrange("f (c e j) -> f c e j", c=2, e=E)[:, :, e, :]

            def one_hot(dst, src, first, n, e):
                return V.tensor_tensor(dst, by_expert(src[:], e).unsqueeze(3).broadcast_to([FH, 2, J, n]),
                                       ci[0:FH, first:first + n].unsqueeze(1).unsqueeze(1).broadcast_to(
                                           [FH, 2, J, n]), ALU.is_equal)

            def hot_high(e):
                if e >= 2:
                    dve.wait_ge(pe_ids, e - 1)
                one_hot(hot_hi[e % 2][:], hi_t, I_HI, HI, e).then_inc(hot_steps, 1)

            def hot_low(e):
                if e >= 1:
                    dve.wait_ge(hot_ready, e)
                one_hot(hot_lo[:], lo_t, I_LO, LO, e).then_inc(hot_steps, 1)
                dve.wait_ge(hot_steps, 2 * e + 2)
                V.tensor_scalar(hot_id[e % 2][:, :, :, 0, :], hot_lo[:], cf[0:FH, C_FROW:C_FROW + 1], None, ALU.mult)
                V.tensor_tensor(hot_id[e % 2][:, :, :, 1, :], hot_lo[:],
                                by_expert(u_bf[:], e).unsqueeze(3).broadcast_to([FH, 2, J, LO]),
                                ALU.mult).then_inc(hot_ready, 1)

            def list_read(e):
                dve.wait_ge(pe_ids, e + 1)
                o = ids_bank.rearrange("h (k l) -> h k l", k=2)
                V.tensor_copy(id_f[:, e, :], o[:, 0, :]).then_inc(id_part, 1)
                dve.wait_ge(id_part, e + 1)
                V.scalar_tensor_tensor(out=id_u[:, e, :], in0=o[:, 1, :], scalar=float(FH), in1=id_f[:, e, :],
                                       op0=ALU.mult, op1=ALU.add).then_inc(ids_ready, 1)

            hot_high(0)
            hot_low(0)
            list_read(0)
            hot_high(1)
            hot_low(1)
            dve.wait_ge(pe_cnt, n_pe + 4)
            V.reciprocal(rz8[:], B6[:, 0:E]).then_inc(topk, 1)
            dve.wait_ge(topk, TK_SLOT + 1)
            list_read(1)
            hot_high(2)
            hot_low(2)
            list_read(2)

            def gated(e, m):
                k = HC * e + m
                dve.wait_ge(a_gate, k + 1)
                if k >= 2:
                    dve.wait_ge(hid_high, k - 1)
                V.tensor_tensor(hid[m % 2][:], gate[k % 2][:], bank[3 + 2 * (k % 2)][:, 0:CAP],
                                ALU.mult).then_inc(hid_ready, 1)

            def hidden_low(e, m):
                dve.wait_ge(hid_high, HC * e + m + 1)
                V.tensor_tensor(hid_lo[e % 2][:, m, :], hid[m % 2][:], hid_hi[e % 2][:, m, :].bitcast(F32),
                                ALU.subtract).then_inc(hid_low, 1)

            def turned_low_parts(e):
                for c in range(DC):
                    dve.wait_ge(a_xgt, DC * e + c + 1)
                    V.tensor_tensor(xg_lo[e % 2][:, c, :], bank[c][:, 0:CAP], xg_hi[e % 2][:, c, :].bitcast(F32),
                                    ALU.subtract).then_inc(x_low, 1)

            def w1_rest(e):
                dve.wait_ge(w1_high, e + 1)
                V.tensor_tensor(w1_lo[e % 2][:], w1_sb[e % NW][:], w1_hi[e % 2][:].bitcast(F32),
                                ALU.subtract).then_inc(w1_low, 1)

            def w3_rest(e):
                dve.wait_ge(w3_high, e + 1)
                V.tensor_tensor(w3_lo[e % 2][:], w3_sb[e % NW][:], w3_hi[e % 2][:].bitcast(F32),
                                ALU.subtract).then_inc(w3_low, 1)

            def slot_weights(e):
                dve.wait_ge(a_exp, e + 1)
                w = w_slot[e % NS]
                V.tensor_scalar(w[:, 0:2, 1], w[:, 0:2, 0], rz8[0:SP_, e:e + 1], None, ALU.mult)
                n = CAP - 2 * SP_
                V.tensor_scalar(w[0:n, 2:3, 1], w[0:n, 2:3, 0], rz8[0:n, e:e + 1], None, ALU.mult).then_inc(w_ready, 1)

            def weighted(e, s):
                n = min(SP_, CAP - s * SP_)
                k = ST * e + s
                if s == 0:
                    dve.wait_ge(w_ready, e + 1)
                    if e >= 2:
                        dve.wait_ge(scattered, 16 * ST * (e - 1))
                dve.wait_ge(pe_y2, k + 1)
                V.tensor_scalar(y_w[e % 2][0:n, s, :], bank[6 + k % 2][0:n, 0:D], w_slot[e % NS][0:n, s, 1:2],
                                None, ALU.mult).then_inc(y_ready, 1)

            turned_low_parts(0)
            gated(0, 0)
            hidden_low(0, 0)
            for e in range(E):
                if e >= 1:
                    slot_weights(e - 1)
                    weighted(e - 1, 0)
                    hidden_low(e, 0)
                if e + NG < E:
                    hot_high(e + NG)
                if e >= 1:
                    weighted(e - 1, 1)
                if e + NG < E:
                    hot_low(e + NG)
                if e >= 1:
                    weighted(e - 1, 2)
                if e + 1 < E:
                    w3_rest(e + 1)
                gated(e, 1)
                if e + NG < E:
                    list_read(e + NG)
                hidden_low(e, 1)
                gated(e, 2)
                if e + 1 < E:
                    turned_low_parts(e + 1)
                hidden_low(e, 2)
                gated(e, 3)
                hidden_low(e, 3)
                if e + 1 < E:
                    gated(e + 1, 0)
            slot_weights(E - 1)
            for s in range(ST):
                weighted(E - 1, s)

        @block.gpsimd
        def _(pool):
            G = nc.gpsimd

            def power(n, t):
                pool.wait_ge(ln[n], LN_STEPS * t.i + 3)
                G.tensor_tensor(rstd[n][t.slot][:], var_eps[n][t.slot][:], neg_half[0:T, :], ALU.pow).then_inc(rs[n], 1)

            def halves(a):
                return a.rearrange("t (n two d) -> t n two d", two=2, d=HD // 2)

            def step(tiles):
                t0, t1, t2, t3, t4 = tiles
                if t2:
                    pool.wait_ge(a_qk, t2.i + 1)
                    if not isinstance(t2.i, int) or t2.i >= 1:
                        pool.wait_ge(roped, ROPE * t2.i)
                    a, b = halves(qk[t2.slot][:]), halves(rope_b[:])
                    for k in range(2):
                        G.tensor_tensor(b[:, :, k, :], a[:, :, 1 - k, :], sines[k], ALU.mult).then_inc(roped, 1)
                    pool.wait_ge(turned, t2.i + 1)
                    pool.wait_ge(roped, ROPE * t2.i + 2)
                    G.tensor_tensor(qkr[t2.slot][:], rope_a[:], rope_b[:], ALU.add).then_inc(roped, 1)
                if t0:
                    power("ln1", t0)
                if t1:
                    power("ln2", t1)
                    power("ln3", t1)
                if t3:
                    power("ln4", t3)

            sines = [sin_t[:, k * HD // 2:(k + 1) * HD // 2].unsqueeze(1).broadcast_to([T, 2 * HEADS, HD // 2])
                     for k in range(2)]
            pool.wait_ge(setup, 1)
            pool.wait_ge(tables_loaded, 16)
            run_steps(pool, step)

            def gather(e):
                pool.wait_ge(ids_in[e % NG], 16 * (e // NG + 1))
                if e >= NG:
                    pool.wait_ge(pe_xgt, DC * (e - NG + 1))
                    pool.wait_ge(a_exp, e - NG + 1)
                for s in range(ST):
                    n = min(SP_, CAP - s * SP_)
                    G.indirect_dma_start(xg[e % NG][0:n, s, :], None, rows_dram,
                                         bass.IndirectOffsetOnAxis(ids[0:n, e, s:s + 1], 0)
                                         ).then_inc(gathered[e % NG], 16)

            def scatter(e):
                for s in range(ST):
                    n = min(SP_, CAP - s * SP_)
                    pool.wait_ge(y_ready, ST * e + s + 1)
                    if e >= 1 and s == 0:
                        pool.wait_ge(scattered, 16 * ST * e)
                    G.indirect_dma_start(out_flat, bass.IndirectOffsetOnAxis(ids[0:n, e, s:s + 1], 0),
                                         y_w[e % 2][0:n, s, :], None, compute_op=ALU.add).then_inc(scattered, 16)

            for k in range(UNROLL):
                n = len(range(k, NT, UNROLL))
                pool.wait_ge(h2_stored[k], 16 * n)
                pool.wait_ge(row_stored[k], 16 * n)

            def rest(e, raw, hi, lo, high, low):
                pool.wait_ge(high, e + 1)
                G.tensor_tensor(lo[e % 2][:], raw[e % NW][:], hi[e % 2][:].bitcast(F32), ALU.subtract).then_inc(low, 1)

            rest(0, w1_sb, w1_hi, w1_lo, w1_high, w1_low)
            rest(0, w3_sb, w3_hi, w3_lo, w3_high, w3_low)
            rest(0, w2_sb, w2_hi, w2_lo, w2_high, w2_low)
            rest(1, w1_sb, w1_hi, w1_lo, w1_high, w1_low)
            for e in range(NG):
                gather(e)
            for e in range(E):
                if e + 1 < E:
                    rest(e + 1, w2_sb, w2_hi, w2_lo, w2_high, w2_low)
                if e + NG < E:
                    gather(e + NG)
                if e + 2 < E:
                    rest(e + 2, w1_sb, w1_hi, w1_lo, w1_high, w1_low)
                scatter(e)
            pool.wait_ge(scattered, 16 * ST * E)


TK_SIGN = 1
TK_MAX = 3
TK_MAXOWN = 13
TK_SEARCH = 13
TK_ROUND = 5
TK_LAST = TK_SEARCH + TK_ROUND * SEARCH + 3
TK_GT = TK_LAST + TK_ROUND + 3
TK_SEL = TK_GT + 4
TK_POS = TK_SEL + 3
TK_Z = TK_POS + 1
TK_SLOT = TK_Z + 2


def constants():
    import numpy as np

    f = np.zeros((P, NC_F), np.float32)
    i = np.zeros((P, NC_I), np.int32)
    f[:, C_ID:C_ID + P] = np.eye(P)
    r = np.arange(T)
    f[:T, C_MASK:C_MASK + T] = (r[:, None] // SEQ == r[None, :] // SEQ) & (r[:, None] <= r[None, :])
    half = HD // 2
    inv = (1.0 / np.float32(10000.0) ** (np.arange(half, dtype=np.float32) / np.float32(half))).astype(np.float32)
    ang = ((r % SEQ).astype(np.float32)[:, None] * inv[None, :]).astype(np.float32)
    scale = np.float32(HD ** -0.25)
    cos, sin = np.cos(ang) * scale, np.sin(ang) * scale
    f[:T, C_COS:C_COS + HD] = np.concatenate([cos, cos], 1)
    f[:T, C_SIN:C_SIN + HD] = np.concatenate([-sin, sin], 1)
    p = np.arange(P)
    f[:, C_HEAD:C_HEAD + HPC] = p[:, None] // HD == np.arange(HPC)[None, :]
    f[:, C_E8:C_E8 + E] = p[:, None] // J == np.arange(E)[None, :]
    for n in range(SEARCH + 1):
        shift = 2 * (HIGH_ROUNDS - 1 - n) if n < HIGH_ROUNDS else 2 * (SEARCH - n) - 1
        f[:, C_SCALE + n] = 2.0 ** max(shift, 0)
        f[:, C_BITS + 3 * n:C_BITS + 3 * n + 3] = np.array([1, 2, 3]) * 2.0 ** max(shift, 0)
    f[:, C_FROW] = p
    i[:, I_HI:I_HI + HI] = np.arange(HI)
    i[:, I_LO:I_LO + LO] = np.arange(LO)
    k = np.arange(2 * P)
    i[:, I_U:I_U + 2 * P] = 2 * (k % J) + k // P
    same = p[:, None] // J == p[None, :] // J
    i[:, I_BLOCK:I_BLOCK + P] = same
    i[:, I_TRI:I_TRI + P] = same & (p[:, None] < p[None, :])
    return f, i


def kernel(**inputs):
    import numpy as np
    import concourse.bacc as bacc
    from concourse.bass_utils import run_bass_kernel_spmd

    x = np.asarray(inputs["x"])
    n_img, chans, height, wide = x.shape
    side = 16
    rows = np.zeros((NT * IMGS, SEQ, PD), x.dtype)
    rows[:n_img, 1:] = x.reshape(n_img, chans, height // side, side, wide // side, side).transpose(
        0, 2, 4, 3, 5, 1).reshape(n_img, SEQ - 1, PD)
    ln2_w, ln2_b = np.asarray(inputs["L0_tok_ln2_w"]), np.asarray(inputs["L0_tok_ln2_b"])
    affine_w = np.zeros((IMGS, SEQ, D), ln2_w.dtype)
    affine_w[:, 1:] = ln2_w
    base = np.zeros((IMGS, SEQ, D), ln2_b.dtype)
    base[:, 1:] = ln2_b
    base[:, 0] = np.asarray(inputs["L0_tok_cls_token"])[0, 0]
    pos = np.tile(np.asarray(inputs["L0_tok_pos_embedding"])[0, :SEQ], (IMGS, 1))
    cf, ci = constants()
    data = {
        "x": rows.reshape(NT, T, PD),
        "consts": cf,
        "consts_i": ci,
        "ln1": np.stack([np.asarray(inputs["L0_tok_ln1_w"]), np.asarray(inputs["L0_tok_ln1_b"])]
                        ).reshape(2, PC, P).transpose(2, 0, 1),
        "lin_w": np.asarray(inputs["L0_tok_lin_w"]),
        "lin_b": np.tile(np.asarray(inputs["L0_tok_lin_b"]), (T, 1)),
        "affine_w": affine_w.reshape(T, D),
        "base": base.reshape(T, D),
        "pos": pos,
        "w_qkv": np.asarray(inputs["L0_attn_w_qkv"]),
        "w_out": np.asarray(inputs["L0_attn_w_out"]),
        "wg": np.asarray(inputs["L0_ffn_Wg"]).T,
        "w1": np.asarray(inputs["L0_ffn_W1"]).transpose(0, 2, 1),
        "w3": np.asarray(inputs["L0_ffn_W3"]).transpose(0, 2, 1),
        "w2": np.asarray(inputs["L0_ffn_W2"]).transpose(0, 2, 1),
    }
    nc = bacc.Bacc("TRN2", target_bir_lowering=False, num_devices=1)
    arrays, args = {}, []
    for name, a in data.items():
        a = np.ascontiguousarray(a)
        arrays[f"in_{name}"] = a
        args.append(nc.dram_tensor(f"in_{name}", a.shape, mybir.dt.from_np(a.dtype), kind="ExternalInput").ap())
    out = nc.dram_tensor("out", (BATCH, SEQ, D), F32, kind="ExternalOutput").ap()
    vit_tower(nc, *args, out)
    r = run_bass_kernel_spmd(nc, [arrays], core_ids=[0])
    return r.results[0]["out"]
```
